# Optimizing a Trainium2 kernel written in Bass

```python
import numpy as np
import jax
import jax.numpy as jnp

def _softmax(x, axis=-1):
    return jax.nn.softmax(x, axis=axis)

def _gelu(x):
    return jax.nn.gelu(x, approximate=True)

def _silu(x):
    return jax.nn.silu(x)

def _sigmoid(x):
    return jax.nn.sigmoid(x)

def _layernorm(x, axis=-1, eps=1e-05):
    m = jnp.mean(x, axis=axis, keepdims=True)
    v = jnp.var(x, axis=axis, keepdims=True)
    return (x - m) / jnp.sqrt(v + eps)

def _scatter_add(tgt, idx, src, axis=0):
    return tgt.at[idx].add(src)

def _segment_sum(src, seg, n):
    return jax.ops.segment_sum(src, seg, n)
kernel_name = 'mk_adj_resnorm_d1_adj_r2_350559'

def setup_inputs(seed: int=0):
    np.random.seed(seed)
    _w = jnp.asarray

    def _rec_inputs():
        import jax
        import jax.numpy as jnp
        _gk = jax.random.key(seed)
        x = -0.006082 + 1.001 * jax.random.normal(jax.random.fold_in(_gk, 1), (32, 256, 64), jnp.float32)
        _a = jax.random.bernoulli(jax.random.fold_in(_gk, 2), 0.0078125, (32, 256, 256))
        _a = jnp.logical_or(_a, jnp.swapaxes(_a, -1, -2))
        _a = jnp.logical_or(_a, jnp.eye(256, dtype=bool))
        _af = _a.astype(jnp.float32)
        _af = _af * jax.random.uniform(jax.random.fold_in(_gk, 3), (32, 256, 256), jnp.float32, 0.05, 4.42607)
        adj = _af
        return (x, adj)
    x, adj = _rec_inputs()

    def _L0_gnn_setup():
        import jax, jax.numpy as jnp
        import numpy as np
        key = jax.random.key(seed)
        ks = jax.random.split(key, 6)
        B, N, F, H, O = (2, 256, 64, 192, 64)
        x = jax.random.normal(ks[0], (B, N, F), dtype=jnp.float32)
        adj = jax.random.normal(ks[1], (B, N, N), dtype=jnp.float32)
        W1 = jax.random.normal(ks[2], (2 * F, H), dtype=jnp.float32) * (1.0 / np.sqrt(2 * F))
        b1 = jax.random.normal(ks[3], (H,), dtype=jnp.float32) * 0.02
        W2 = jax.random.normal(ks[4], (H, O), dtype=jnp.float32) * (1.0 / np.sqrt(H))
        b2 = jax.random.normal(ks[5], (O,), dtype=jnp.float32) * 0.02
        return {'x': x, 'adj': adj, 'W1': W1, 'b1': b1, 'W2': W2, 'b2': b2}
    _L0_gnn_all = _L0_gnn_setup()
    _L0_gnn_in = {k: v for k, v in _L0_gnn_all.items() if k in ('W1', 'b1', 'W2', 'b2')}
    del _L0_gnn_all
    return {'x': x, 'adj': adj, 'L0_gnn_W1': _L0_gnn_in['W1'], 'L0_gnn_b1': _L0_gnn_in['b1'], 'L0_gnn_W2': _L0_gnn_in['W2'], 'L0_gnn_b2': _L0_gnn_in['b2']}

def reference(x, adj, L0_gnn_W1, L0_gnn_b1, L0_gnn_W2, L0_gnn_b2):
    import jax
    import jax.numpy as jnp

    def _L0_gnn_ref(x, adj, W1, b1, W2, b2):
        import jax, jax.numpy as jnp
        import numpy as np
        F = x.shape[-1]
        mask = (adj > 0.0).astype(x.dtype)
        W1a, W1b = (W1[:F], W1[F:])
        xj_proj = x @ W1a
        diff = x[:, :, None, :] - x[:, None, :, :]
        h = jax.nn.relu(xj_proj[:, :, None, :] + diff @ W1b + b1)
        hm = jnp.einsum('bjkh,bjk->bjh', h, mask)
        deg = jnp.sum(mask, axis=-1)
        return hm @ W2 + deg[..., None] * b2
    x = _layernorm(x + _L0_gnn_ref(x, adj, L0_gnn_W1, L0_gnn_b1, L0_gnn_W2, L0_gnn_b2), axis=-1)
    return x

_drawn_inputs = setup_inputs


def setup_inputs(seed=0):
    import zlib

    import numpy as np

    out = dict(_drawn_inputs(seed))
    spreads = {}
    factors = {'L0_gnn_b1': 3.735}
    for name, (base, spread) in spreads.items():
        noise = np.random.default_rng([zlib.crc32(name.encode()), seed]).standard_normal(out[name].shape)
        drawn = base * np.exp(spread * noise) if base else spread * noise
        out[name] = jnp.asarray(drawn.astype(out[name].dtype))
    for name, factor in factors.items():
        out[name] = (out[name] * factor).astype(out[name].dtype)
    return out
```

```python
from contextlib import ExitStack

import numpy as np

import concourse.bass as bass
from concourse import mybir

ALU = mybir.AluOpType
ACT = mybir.ActivationFunctionType
F32 = mybir.dt.float32
BF16 = mybir.dt.bfloat16
F16 = mybir.dt.float16
I32 = mybir.dt.int32
AX = mybir.AxisListType

GRAPHS, N, F, H, O = 32, 256, 64, 192, 64
EPS = 1e-5
P = 128
NT = N // P
PAIRS = GRAPHS // 2
HT = H - P
TILES = 2 * NT
MARK = 2 * N

SMALL, NSMALL = 16, 8
CAPS = [256, 256, 256, 224, 184, 128, 88, 48, 48] + [SMALL] * NSMALL
START = [sum(CAPS[:s]) for s in range(len(CAPS))]
COLS = sum(CAPS)
BIG_SLOTS = len(CAPS) - NSMALL


def slots_given(rank):
    return sum(c > rank for c in CAPS)


UNITS = [
    ("main", 0, 1, [(0, 1)]),
    ("tail", 0, 2, [(0, 2)]),
    ("main", 1, 2, [(1, 1)]),
    ("tail", 2, 4, [(2, 1), (3, 1)]),
    ("main", 2, 3, [(2, 1)]),
    ("tail", 4, 7, [(4, 1), (5, 1), (6, 1)]),
    ("main", 3, 4, [(3, 1)]),
    ("main", 4, 5, [(4, 1)]),
    ("tail", 7, 17, [(7, 2), (9, 8)]),
    ("main", 5, 7, [(5, 1), (6, 1)]),
    ("main", 7, 17, [(7, 2), (9, 8)]),
]
NU = len(UNITS)
BANKS = 3


def unit_cols(unit):
    _, s0, s1, _ = UNITS[unit]
    return START[s0], sum(CAPS[s0:s1])


def adds_of(unit):
    return sum(1 if s0 >= BIG_SLOTS else n for s0, n in UNITS[unit][3])


SHIFTS = [len(u[3]) for u in UNITS]
SHIFTS_BEFORE = [sum(SHIFTS[:u]) for u in range(NU + 1)]
ADDS_BEFORE = [sum(adds_of(i) for i in range(u)) for u in range(NU + 1)]
NSHIFT, NADD = SHIFTS_BEFORE[NU], ADDS_BEFORE[NU]
NHOT = BIG_SLOTS + 1

GENERAL_STEPS = 7

CONSTS = {}


def constants():
    p = np.arange(P)[:, None]
    node = np.arange(TILES * P)[None, :] % N
    parts = dict(
        ident=np.eye(P),
        iota=np.broadcast_to(np.arange(N)[None, :], (P, N)),
        tie_row=np.broadcast_to((N - 1 - node) / N, (P, 2 * N)),
        tie_col=(N - 1 - (np.arange(TILES)[None, :] % NT * P + p)) / N,
        neg_given=np.broadcast_to([-slots_given(r) for r in range(N)] * 2, (P, 2 * N)),
        before=(p < np.arange(P)[None, :]) + MARK * np.eye(P),
        small_marks=np.broadcast_to(
            np.repeat(MARK + BIG_SLOTS + np.arange(NSMALL), SMALL)[None, :], (P, NSMALL * SMALL)),
        marks=np.broadcast_to(MARK + np.arange(N)[None, :], (P, N)),
        eps=np.full((P, 1), EPS),
    )
    at = 0
    for name, a in parts.items():
        CONSTS[name] = (at, a.shape[1])
        at += a.shape[1]
    return np.ascontiguousarray(np.concatenate(list(parts.values()), axis=1).astype(np.float32))


class Pair:

    def __init__(self, i, offset, general=False):
        base = PAIRS if general else 0
        self.n = 2 * i + (offset + base)
        self.half = i + (offset + base) // 2
        self.side = offset % 2
        self.data = 2 * i + offset
        self.general = general
        self.i, self.offset = i, offset

    def follows(self, k):
        return not isinstance(self.n, int) or self.n >= k

    def next(self):
        return Pair(self.i, self.offset + 1, self.general)

    def prev(self):
        return Pair(self.i, self.offset - 1, self.general)


def build(nc, x, xT, adj, w1, b1, w2, b2, consts, out):
    x_v = x.rearrange("(g two) (t p) f -> g p (two t) f", two=2, p=P)
    adj_v = adj.rearrange("(g two) (t p) k -> g p (two t) k", two=2, p=P)
    out_v = out.rearrange("(g two) (t p) f -> g p (two t) f", two=2, p=P)
    xT_v = xT.rearrange("f (g n) -> g f n", n=2 * N)

    with ExitStack() as ctx:
        def sb(name, shape, dt=F32):
            return ctx.enter_context(nc.sbuf_tensor(name, shape, dt))

        def bank(name):
            return ctx.enter_context(nc.psum_tensor(name, [P, 512], F32))

        def sem(name):
            return ctx.enter_context(nc.semaphore(name))

        def both(name, shape, dt=F32):
            return [sb(f"{name}{s}", shape, dt) for s in range(2)]

        cst = sb("cst", [P, consts.shape[1]])

        def const(name):
            at, n = CONSTS[name]
            return cst[:, at:at + n]

        ident = sb("ident", [P, P], BF16)
        iota = sb("iota", [P, N], BF16)
        tie_row = sb("tie_row", [P, 2 * N], BF16)
        neg_given = sb("neg_given", [P, 2 * N], BF16)
        before = sb("before", [P, P], BF16)
        ones = sb("ones", [P, P], BF16)
        small_marks = sb("small_marks", [P, NSMALL * SMALL], F16)
        w1a = sb("w1a", [F, H])
        w1b = sb("w1b", [F, H])
        w1ab = sb("w1ab", [F, H])
        w1n = sb("w1n", [F, H])
        b1m = sb("b1m", [P, 1])
        b1t = sb("b1t", [P, 1])
        w2m = sb("w2m", [P, O])
        w2t = sb("w2t", [P, 2, O])
        b2r = sb("b2r", [1, O])
        adj_sb = both("adj_sb", [P, TILES, N])
        x_sb = both("x_sb", [P, TILES, F])
        xT_sb = both("xT_sb", [F, 2 * N])
        mask = both("mask", [P, TILES, N], BF16)
        deg = both("deg", [P, TILES])
        deg16 = both("deg16", [P, TILES], BF16)
        key = sb("key", [P, TILES])
        rank = sb("rank", [P, TILES])
        junk = sb("junk", [P, TILES, N], BF16)
        perm = both("perm", [P, TILES, N], BF16)
        permT = sb("permT", [P, TILES, N])
        maskT = sb("maskT", [P, TILES, N], BF16)
        slotT = sb("slotT", [P, TILES, N], F16)
        hot = both("hot", [P, TILES, COLS], BF16)
        excess = sb("excess", [1, 2 * N])
        excess_junk = sb("excess_junk", [1, 2 * N])
        over = sb("over", [1, 1])
        over_sum = sb("over_sum", [1, 1])
        over_int = sb("over_int", [1, 1], I32)
        deg_row = both("deg_row", [1, 2 * N])
        xh = sb("xh", [P, TILES, F], BF16)
        xm = sb("xm", [P, TILES, F], BF16)
        xl = sb("xl", [P, TILES, F], BF16)
        xr = sb("xr", [P, TILES, F])
        xs = sb("xs", [F, 2 * N])
        vr = sb("vr", [P, TILES, H])
        vh = both("vh", [P, TILES, H], BF16)
        vm = both("vm", [P, TILES, H], BF16)
        vl = both("vl", [P, TILES, H], BF16)
        um = both("um", [P, 2, N])
        ut = both("ut", [P, N])
        sm = both("sm", [P, 2, N])
        st = both("st", [P, N])
        NTMP = 3
        tmp = [sb(f"tmp{i}", [P, 512]) for i in range(NTMP)]
        small_sum = sb("small_sum", [P, 2, SMALL])
        y_sb = sb("y_sb", [P, TILES, O])
        z = sb("z", [P, TILES, O])
        stats = sb("stats", [P, TILES, 6])
        apart, within, across = sb("apart", [P, TILES]), sb("within", [P, TILES]), sb("across", [P, TILES])
        mean = sb("mean", [P, TILES])
        spread = sb("spread", [P, TILES])
        std = sb("std", [P, TILES])
        rstd = sb("rstd", [P, TILES])
        idle = sb("idle", [P, 1])
        o_sb = both("o_sb", [P, TILES, O])

        bx0, bx1, bx2, bx3 = (bank(f"bx{i}") for i in range(4))
        by = bank("by")
        ring = [bank(f"ring{i}") for i in range(BANKS)]

        consts_loaded, weights_loaded = sem("consts_loaded"), sem("weights_loaded")
        consts_ready, weights_ready = sem("consts_ready"), sem("weights_ready")
        adj_loaded = [sem(f"adj_loaded{s}") for s in range(2)]
        x_loaded = [sem(f"x_loaded{s}") for s in range(2)]
        xT_loaded = [sem(f"xT_loaded{s}") for s in range(2)]
        stored = [sem(f"stored{s}") for s in range(2)]
        masks_ready = sem("masks_ready")
        degrees_ready = sem("degrees_ready")
        keys_ready = sem("keys_ready")
        ranks_ready = sem("ranks_ready")
        perm_ready = sem("perm_ready")
        maskT_ready = sem("maskT_ready")
        maskT_copied = sem("maskT_copied")
        slots_ready = sem("slots_ready")
        slots_copied = sem("slots_copied")
        excess_ready = sem("excess_ready")
        excess_copied = sem("excess_copied")
        over_ready = sem("over_ready")
        over_added = sem("over_added")
        deg_row_ready = sem("deg_row_ready")
        xh_ready, xr_ready = sem("xh_ready"), sem("xr_ready")
        xm_ready, xl_ready = sem("xm_ready"), sem("xl_ready")
        xs_ready, xs_copied = sem("xs_ready"), sem("xs_copied")
        u_ready, u_copied = sem("u_ready"), sem("u_copied")
        v_ready, vh_ready = sem("v_ready"), sem("vh_ready")
        vr_ready, vm_ready, vl_ready = sem("vr_ready"), sem("vm_ready"), sem("vl_ready")
        sums_started = sem("sums_started")
        hot_ready = sem("hot_ready")
        gathered = sem("gathered")
        shifted = sem("shifted")
        clamped, reduced = sem("clamped"), sem("reduced")
        added = sem("added")
        permT_ready, permT_copied = sem("permT_ready"), sem("permT_copied")
        y_ready, y_copied = sem("y_ready"), sem("y_copied")
        z_ready, z_added = sem("z_ready"), sem("z_added")
        stats_ready, moments_ready = sem("stats_ready"), sem("moments_ready")
        std_ready, rstd_ready = sem("std_ready"), sem("rstd_ready")
        normed = sem("normed")
        over_all = sem("over_all")
        general_hot, general_gathered = sem("general_hot"), sem("general_gathered")
        general_step = sem("general_step")

        block = ctx.enter_context(nc.Block())

        def general_loop(eng, body, after=None):
            eng.wait_ge(over_all, 1)
            needed = eng.value_load(over_int[0:1, 0:1], min_val=0, max_val=GRAPHS * N * N)
            with eng.If(needed > 0):
                with eng.Fori(0, PAIRS // 2) as i:
                    for side in range(2):
                        pair = Pair(i, side, general=True)
                        eng.wait_ge(normed, pair.n)
                        body(pair)
                if after:
                    after()

        @block.sync
        def _(eng):
            eng.dma_start(cst[:, :], consts[:, :]).then_inc(consts_loaded, 16)

            def load_adj(pair):
                if not pair.general and pair.follows(2):
                    eng.wait_ge(masks_ready, pair.n - 1)
                eng.dma_start(adj_sb[pair.side][:, :, :], adj_v[pair.data]).then_inc(adj_loaded[pair.side], 16)

            def load_xT(pair):
                if not pair.general and pair.follows(2):
                    eng.wait_ge(v_ready, 2 * (pair.n - 1))
                eng.dma_start(xT_sb[pair.side][:, :], xT_v[pair.data]).then_inc(xT_loaded[pair.side], 16)

            def load_x(pair):
                if not pair.general and pair.follows(2):
                    eng.wait_ge(z_added, pair.n - 1)
                eng.dma_start(x_sb[pair.side][:, :, :], x_v[pair.data]).then_inc(x_loaded[pair.side], 16)

            def store(pair):
                eng.wait_ge(normed, pair.n + 1)
                eng.dma_start(out_v[pair.data], o_sb[pair.side][:, :, :]).then_inc(stored[pair.side], 16)

            def body(pair, first=False, ahead=2):
                if ahead == 2:
                    load_adj(pair.next().next())
                    load_xT(pair.next().next())
                if ahead >= 1:
                    load_x(pair.next())
                if not first:
                    store(pair.prev())

            load_adj(Pair(0, 0))
            load_x(Pair(0, 0))
            eng.dma_start(w1a[:, :], w1[0:F, :]).then_inc(weights_loaded, 16)
            eng.dma_start(w1b[:, :], w1[F:2 * F, :]).then_inc(weights_loaded, 16)
            for half in range(2):
                rows = slice(half * HT, half * HT + HT)
                eng.dma_start(b1t[rows, :], b1[P:H].rearrange("(h one) -> h one", one=1)).then_inc(weights_loaded, 16)
                eng.dma_start(w2t[rows, half, :], w2[P:H, :]).then_inc(weights_loaded, 16)
            eng.dma_start(b1m[:, :], b1[0:P].rearrange("(h one) -> h one", one=1)).then_inc(weights_loaded, 16)
            eng.dma_start(w2m[:, :], w2[0:P, :]).then_inc(weights_loaded, 16)
            eng.dma_start(b2r[:, :], b2.rearrange("(one o) -> one o", one=1)).then_inc(weights_loaded, 16)
            load_xT(Pair(0, 0))
            load_adj(Pair(0, 1))
            load_xT(Pair(0, 1))
            body(Pair(0, 0), first=True)
            body(Pair(0, 1))
            with eng.Fori(1, (PAIRS - 2) // 2) as i:
                body(Pair(i, 0))
                body(Pair(i, 1))
            body(Pair(0, PAIRS - 2), ahead=1)
            body(Pair(0, PAIRS - 1), ahead=0)
            store(Pair(0, PAIRS - 1))
            for side in range(2):
                eng.wait_ge(stored[side], 16 * (PAIRS // 2))

            def general(pair):
                load_adj(pair)
                load_xT(pair)
                load_x(pair)
                store(pair)

            def all_stored():
                for side in range(2):
                    eng.wait_ge(stored[side], 16 * PAIRS)

            general_loop(eng, general, all_stored)

        @block.gpsimd
        def _(eng):
            def split_x(pair):
                eng.wait_ge(xh_ready, pair.n + 1)
                if pair.follows(1):
                    eng.wait_ge(xm_ready, pair.n)
                eng.tensor_tensor(xr[:, :, :], x_sb[pair.side][:, :, :], xh[:, :, :],
                                  ALU.subtract).then_inc(xr_ready, 1)
                eng.wait_ge(xm_ready, pair.n + 1)
                eng.wait_ge(xr_ready, pair.n + 1)
                eng.tensor_tensor(xl[:, :, :], xr[:, :, :], xm[:, :, :], ALU.subtract).then_inc(xl_ready, 1)

            def row_of_degrees(pair):
                eng.wait_ge(excess_copied, pair.n + 1)
                if pair.follows(2):
                    eng.wait_ge(y_ready, pair.n - 1)
                if pair.general:
                    eng.tensor_tensor(deg_row[pair.side][:, :], excess[:, :],
                                      ones[0:1, 0:1].to_broadcast([1, 2 * N]), ALU.mult).then_inc(deg_row_ready, 1)
                    return
                eng.tensor_tensor(deg_row[pair.side][:, :], excess[:, :], neg_given[0:1, :],
                                  ALU.subtract).then_inc(deg_row_ready, 1)
                eng.wait_ge(over_ready, pair.n + 1)
                eng.wait_ge(over_added, pair.n + 1)
                eng.tensor_tensor(over_sum[:, :], over_sum[:, :], over[:, :], ALU.add).then_inc(over_added, 1)

            def split_v(pair, g):
                eng.wait_ge(vm_ready, 2 * pair.n + g + 1)
                if not pair.general and pair.follows(2):
                    eng.wait_ge(gathered, NU * (pair.n - 1))
                c = slice(g * NT, g * NT + NT)
                eng.tensor_tensor(vl[pair.side][:, c, :], vr[:, c, :], vm[pair.side][:, c, :],
                                  ALU.subtract).then_inc(vl_ready, 1)

            def prepare(pair):
                split_x(pair)
                row_of_degrees(pair)
                split_v(pair, 0)
                split_v(pair, 1)

            eng.wait_ge(consts_ready, 7)
            prepare(Pair(0, 0))
            prepare(Pair(0, 1))
            with eng.Fori(1, PAIRS // 2) as i:
                prepare(Pair(i, 0))
                prepare(Pair(i, 1))
            eng.wait_ge(over_added, PAIRS + 1)
            eng.tensor_copy(over_int[:, :], over_sum[:, :]).then_inc(over_all, 1)
            general_loop(eng, prepare)

        @block.scalar
        def _(eng):
            eng.wait_ge(consts_loaded, 16)
            for to, name in ((ident, "ident"), (iota, "iota"), (tie_row, "tie_row"), (neg_given, "neg_given"),
                             (before, "before"), (small_marks, "small_marks")):
                eng.copy(to[:, :], const(name)).then_inc(consts_ready, 1)
            eng.wait_ge(weights_loaded, 16 * 9)
            eng.mul(w1n[:, :], w1b[:, :], -1.0).then_inc(weights_ready, 1)

            def high_x(pair):
                eng.wait_ge(x_loaded[pair.side], 16 * (pair.half + 1))
                if pair.follows(1):
                    eng.wait_ge(xs_ready, pair.n)
                eng.copy(xh[:, :, :], x_sb[pair.side][:, :, :]).then_inc(xh_ready, 1)

            def middle_x(pair):
                eng.wait_ge(xr_ready, pair.n + 1)
                eng.copy(xm[:, :, :], xr[:, :, :]).then_inc(xm_ready, 1)

            def copy_maskT(pair):
                for g, b in enumerate((bx1, bx2)):
                    eng.wait_ge(maskT_ready, 2 * pair.n + g + 1)
                    if pair.follows(1):
                        eng.wait_ge(slots_ready, 2 * (pair.n - 1) + g + 1)
                    eng.copy(maskT[:, g * NT:g * NT + NT, :].rearrange("p t r -> p (t r)"),
                             b[:, :]).then_inc(maskT_copied, 1)

            def copy_slots(pair):
                if not pair.general and pair.follows(1):
                    eng.wait_ge(hot_ready, NHOT * pair.n)
                for g, b in enumerate((bx0, bx1)):
                    eng.wait_ge(slots_ready, 2 * pair.n + g + 1)
                    eng.copy(slotT[:, g * NT:g * NT + NT, :].rearrange("p t r -> p (t r)"),
                             b[:, :]).then_inc(slots_copied, 1)

            def copy_excess(pair):
                eng.wait_ge(excess_ready, pair.n + 1)
                if pair.follows(1):
                    eng.wait_ge(deg_row_ready, pair.n)
                eng.copy(excess[:, :], bx3[0:1, :]).then_inc(excess_copied, 1)
                if not pair.general:
                    eng.wait_ge(excess_copied, pair.n + 1)
                    eng.wait_ge(over_added, pair.n + 1)
                    eng.activation(excess_junk[:, :], excess[:, :], ACT.Relu,
                                   accum_out=over[:, :]).then_inc(over_ready, 1)

            def copy_xs(pair):
                eng.wait_ge(xs_ready, pair.n + 1)
                if pair.follows(1):
                    eng.wait_ge(u_ready, 2 * pair.n)
                eng.copy(xs[:, :], bx2[0:F, :]).then_inc(xs_copied, 1)

            def copy_u(pair):
                if not pair.general and pair.follows(2):
                    eng.wait_ge(shifted, NSHIFT * (pair.n - 1))
                eng.wait_ge(u_ready, 2 * pair.n + 1)
                eng.activation(um[pair.side][:, :, :].rearrange("p g r -> p (g r)"), bx0[:, :], ACT.Identity,
                               bias=b1m[:, 0:1]).then_inc(u_copied, 1)
                eng.wait_ge(u_ready, 2 * pair.n + 2)
                eng.activation(ut[pair.side][:, :], bx1[:, 0:N], ACT.Identity,
                               bias=b1t[:, 0:1]).then_inc(u_copied, 1)

            def high_v(pair, g):
                eng.wait_ge(v_ready, 2 * pair.n + g + 1)
                if not pair.general and pair.follows(2):
                    eng.wait_ge(gathered, NU * (pair.n - 1))
                b = (bx2, bx1)[g]
                eng.copy(vh[pair.side][:, g * NT:g * NT + NT, :].rearrange("p t h -> p (t h)"),
                         b[:, 0:NT * H]).then_inc(vh_ready, 1)

            def middle_v(pair, g):
                eng.wait_ge(vr_ready, 2 * pair.n + g + 1)
                eng.copy(vm[pair.side][:, g * NT:g * NT + NT, :],
                         vr[:, g * NT:g * NT + NT, :]).then_inc(vm_ready, 1)

            def copy_permT(pair):
                eng.wait_ge(permT_ready, pair.n + 1)
                if pair.follows(1):
                    eng.wait_ge(z_ready, pair.n)
                eng.copy(permT[:, :, :].rearrange("p t n -> p (t n)"), bx3[:, :].bitcast(BF16)).then_inc(permT_copied, 1)

            def copy_y(pair):
                eng.wait_ge(y_ready, pair.n + 1)
                if pair.follows(1):
                    eng.wait_ge(z_ready, pair.n)
                eng.copy(y_sb[:, :, :].rearrange("p t o -> p (t o)"), by[:, 0:TILES * O]).then_inc(y_copied, 1)

            def deviation(pair):
                eng.wait_ge(moments_ready, 5 * (pair.n + 1))
                if pair.follows(1):
                    eng.wait_ge(rstd_ready, pair.n)
                eng.activation(std[:, :], spread[:, :], ACT.Sqrt, scale=1.0 / O,
                               bias=const("eps")).then_inc(std_ready, 1)

            def body(pair, prepare=True, finish=True):
                if prepare:
                    new = pair.next()
                if finish:
                    old = pair.prev()
                    copy_permT(old)
                    copy_y(old)
                if prepare:
                    high_x(new)
                    middle_x(new)
                    copy_maskT(new)
                if finish:
                    deviation(old)
                if prepare:
                    copy_excess(new)
                    copy_slots(new)
                    copy_xs(new)
                    copy_u(new)
                    high_v(new, 0)
                    high_v(new, 1)
                    middle_v(new, 0)
                    middle_v(new, 1)

            body(Pair(0, -1), finish=False)
            body(Pair(0, 0), finish=False)
            body(Pair(0, 1))
            with eng.Fori(1, PAIRS // 2 - 1) as i:
                body(Pair(i, 0))
                body(Pair(i, 1))
            body(Pair(0, PAIRS - 2))
            body(Pair(0, PAIRS - 1), prepare=False)
            body(Pair(0, PAIRS), prepare=False)

            def general(pair):
                body(pair.prev(), finish=False)
                body(pair.next(), prepare=False)

            general_loop(eng, general)

        @block.tensor
        def _(eng):
            eng.wait_ge(consts_ready, 7)
            eng.wait_ge(weights_ready, 4)

            def keys(pair):
                eng.wait_ge(degrees_ready, 2 * (pair.n + 1))
                if pair.follows(1):
                    eng.wait_ge(u_copied, 2 * pair.n)
                for c in range(TILES):
                    eng.matmul(bx0[:, c * P:c * P + P], deg16[pair.side][:, c:c + 1].to_broadcast([P, P]),
                               ident[:, :], start=True, stop=False)
                    last = eng.matmul(bx0[:, c * P:c * P + P], ones[0:1, :], tie_row[0:1, c * P:c * P + P],
                                      start=False, stop=True)
                last.then_inc(keys_ready, 1)

            def turn_masks(pair):
                eng.wait_ge(perm_ready, pair.n + 1)
                if pair.follows(1):
                    eng.wait_ge(vr_ready, 2 * pair.n)
                for g, b in enumerate((bx1, bx2)):
                    for k in range(NT):
                        for t in range(NT):
                            last = eng.matmul(b[:, k * N:k * N + N], mask[pair.side][:, g * NT + t, k * P:k * P + P],
                                              perm[pair.side][:, g * NT + t, :], start=(t == 0), stop=(t == NT - 1))
                    last.then_inc(maskT_ready, 1)

            def excesses(pair):
                if pair.general:
                    if pair.follows(1):
                        eng.wait_ge(permT_copied, pair.n)
                else:
                    if pair.follows(2):
                        eng.wait_ge(permT_copied, pair.n - 1)
                for g in range(2):
                    for t in range(NT):
                        last = eng.matmul(bx3[:, g * N:g * N + N],
                                          deg16[pair.side][:, g * NT + t:g * NT + t + 1].to_broadcast([P, P]),
                                          perm[pair.side][:, g * NT + t, :], start=(t == 0),
                                          stop=(pair.general and t == NT - 1))
                    if not pair.general:
                        last = eng.matmul(bx3[:, g * N:g * N + N], ones[0:1, :], neg_given[0:1, g * N:g * N + N],
                                          start=False, stop=True)
                last.then_inc(excess_ready, 1)

            def number_slots(pair):
                for g, b in enumerate((bx0, bx1)):
                    eng.wait_ge(maskT_copied, 2 * pair.n + g + 1)
                    eng.matmul(b[:, 0:N], before[:, :], maskT[:, g * NT, :], start=True, stop=True)
                    eng.matmul(b[:, N:2 * N], ones[:, :], maskT[:, g * NT, :], start=True, stop=False)
                    eng.matmul(b[:, N:2 * N], before[:, :], maskT[:, g * NT + 1, :], start=False,
                               stop=True).then_inc(slots_ready, 1)

            def sort_x(pair):
                eng.wait_ge(xl_ready, pair.n + 1)
                eng.wait_ge(maskT_copied, 2 * pair.n + 2)
                steps = [(t, part) for t in range(NT) for part in (xh, xm, xl)]
                for g in range(2):
                    for s, (t, part) in enumerate(steps):
                        last = eng.matmul(bx2[0:F, g * N:g * N + N], part[:, g * NT + t, :],
                                          perm[pair.side][:, g * NT + t, :], start=(s == 0),
                                          stop=(s == len(steps) - 1))
                last.then_inc(xs_ready, 1)

            def hidden_u(pair):
                eng.wait_ge(xs_copied, pair.n + 1)
                eng.wait_ge(slots_copied, 2 * pair.n + 2)
                eng.matmul(bx0[:, :], w1ab[:, 0:P], xs[:, :], start=True, stop=True).then_inc(u_ready, 1)
                for g in range(2):
                    last = eng.matmul(bx1[g * HT:g * HT + HT, 0:N], w1ab[:, P:H], xs[:, g * N:g * N + N],
                                      start=True, stop=True, skip_group_check=True)
                last.then_inc(u_ready, 1)

            def hidden_v(pair, g):
                eng.wait_ge(xT_loaded[pair.side], 16 * (pair.half + 1))
                if g == 1:
                    eng.wait_ge(u_copied, 2 * pair.n + 2)
                b = (bx2, bx1)[g]
                for t in range(NT):
                    last = eng.matmul(b[:, t * H:t * H + H], xT_sb[pair.side][:, (g * NT + t) * P:(g * NT + t + 1) * P],
                                      w1n[0:F, :], start=True, stop=True)
                last.then_inc(v_ready, 1)

            def turn_perm(pair, next_started=True):
                eng.wait_ge(perm_ready, pair.n + 1)
                eng.wait_ge(sums_started, 3 * (pair.n + (2 if next_started else 1)))
                eng.wait_ge(excess_copied, pair.n + (2 if next_started else 1))
                to = bx3[:, :].bitcast(BF16)
                for g in range(2):
                    for r in range(NT):
                        for t in range(NT):
                            at = (g * NT + r) * N + t * P
                            last = eng.transpose(to[:, at:at + P], perm[pair.side][:, g * NT + t, r * P:r * P + P],
                                                 ident[:, :])
                last.then_inc(permT_ready, 1)

            def project(pair):
                if pair.general:
                    eng.wait_ge(general_step, (pair.data + 1) * (N * GENERAL_STEPS))
                else:
                    eng.wait_ge(added, NADD * (pair.n + 1))
                eng.wait_ge(deg_row_ready, pair.n + 1)
                if pair.follows(1):
                    eng.wait_ge(z_added, pair.n)
                for g in range(2):
                    for r in range(NT):
                        to = by[:, (g * NT + r) * O:(g * NT + r + 1) * O]
                        cols = slice(r * P, r * P + P)
                        eng.matmul(to, sm[pair.side][:, g, cols], w2m[:, :], start=True, stop=False)
                        eng.matmul(to, st[pair.side][:, cols], w2t[:, g, :], start=False, stop=False)
                        last = eng.matmul(to, deg_row[pair.side][0:1, g * N + r * P:g * N + r * P + P], b2r[:, :],
                                          start=False, stop=True)
                last.then_inc(y_ready, 1)

            def unsort_y(pair):
                eng.wait_ge(y_copied, pair.n + 1)
                eng.wait_ge(permT_copied, pair.n + 1)
                for g in range(2):
                    for t in range(NT):
                        at = TILES * O + (g * NT + t) * O
                        for r in range(NT):
                            last = eng.matmul(by[:, at:at + O], permT[:, g * NT + r, t * P:t * P + P],
                                              y_sb[:, g * NT + r, :], start=(r == 0), stop=(r == NT - 1))
                last.then_inc(z_ready, 1)

            def gather_into(side, b, tile, selection, n):
                steps = [(k, part) for k in range(NT) for part in (vh, vm, vl)]
                if tile == "main":
                    for g in range(2):
                        for s, (k, part) in enumerate(steps):
                            last = eng.matmul(b[:, g * n:g * n + n], part[side][:, g * NT + k, 0:P],
                                              selection(g * NT + k), start=(s == 0), stop=(s == len(steps) - 1))
                else:
                    for s, (k, part) in enumerate(steps):
                        for g in range(2):
                            last = eng.matmul(b[g * HT:g * HT + HT, 0:n], part[side][:, g * NT + k, P:H],
                                              selection(g * NT + k), start=(s == 0), stop=(s == len(steps) - 1),
                                              skip_group_check=True)
                return last

            def gather(pair, unit):
                tile, s0, s1, _ = UNITS[unit]
                c0, n = unit_cols(unit)
                if unit == 0:
                    eng.wait_ge(vl_ready, 2 * (pair.n + 1))
                eng.wait_ge(hot_ready, NHOT * pair.n + min(s1, NHOT))
                if unit >= BANKS:
                    eng.wait_ge(shifted, NSHIFT * pair.n + SHIFTS_BEFORE[unit - BANKS + 1])
                else:
                    before_it = max(u for u in range(NU) if u % BANKS == unit)
                    if pair.follows(1):
                        eng.wait_ge(shifted, NSHIFT * (pair.n - 1) + SHIFTS_BEFORE[before_it + 1])
                b = ring[unit % BANKS]
                gather_into(pair.side, b, tile, lambda c: hot[pair.side][:, c, c0:c0 + n], n).then_inc(gathered, 1)

            def prepare_all(pair):
                keys(pair)
                turn_masks(pair)
                excesses(pair)
                number_slots(pair)
                sort_x(pair)
                hidden_u(pair)
                hidden_v(pair, 0)
                hidden_v(pair, 1)

            def body(pair, prepare=True, finish=True):
                new = pair.next()
                old = pair.prev()
                gather(pair, 0)
                gather(pair, 1)
                if finish:
                    turn_perm(old)
                    project(old)
                if prepare:
                    keys(new)
                gather(pair, 2)
                gather(pair, 3)
                if finish:
                    unsort_y(old)
                if prepare:
                    turn_masks(new)
                    excesses(new)
                gather(pair, 4)
                if prepare:
                    number_slots(new)
                    sort_x(new)
                gather(pair, 5)
                if prepare:
                    hidden_u(new)
                    hidden_v(new, 0)
                gather(pair, 6)
                if prepare:
                    hidden_v(new, 1)
                for unit in range(7, NU):
                    gather(pair, unit)

            prepare_all(Pair(0, 0))
            body(Pair(0, 0), finish=False)
            body(Pair(0, 1))
            with eng.Fori(1, PAIRS // 2 - 1) as i:
                body(Pair(i, 0))
                body(Pair(i, 1))
            body(Pair(0, PAIRS - 2))
            body(Pair(0, PAIRS - 1), prepare=False)
            last_pair = Pair(0, PAIRS - 1)
            turn_perm(last_pair, next_started=False)
            project(last_pair)
            unsort_y(last_pair)

            def general(pair):
                prepare_all(pair)
                with eng.Fori(0, N) as s:
                    eng.wait_ge(vl_ready, 2 * (pair.n + 1))
                    eng.wait_ge(general_hot, pair.data * N + s + 1)
                    gather_into(pair.side, ring[0], "main", lambda c: hot[0][:, c, 0:N], N)
                    gather_into(pair.side, ring[1], "tail", lambda c: hot[0][:, c, 0:N], N
                                ).then_inc(general_gathered, 1)
                project(pair)
                turn_perm(pair, next_started=False)
                unsort_y(pair)

            general_loop(eng, general)

        @block.vector
        def _(eng):
            eng.memset(over_sum[:, :], 0.0).then_inc(over_added, 1)
            for half in range(2):
                other = slice((1 - half) * HT, (2 - half) * HT)
                eng.memset(w2t[other, half, :], 0.0).then_inc(weights_ready, 1)
            eng.memset(ones[:, :], 1.0).then_inc(consts_ready, 1)
            eng.wait_ge(weights_loaded, 16 * 9)
            eng.tensor_tensor(w1ab[:, :], w1a[:, :], w1b[:, :], ALU.add).then_inc(weights_ready, 1)
            eng.wait_ge(consts_ready, 7)

            def masks(pair):
                eng.wait_ge(adj_loaded[pair.side], 16 * (pair.half + 1))
                if pair.follows(2):
                    eng.wait_ge(excess_ready, pair.n - 1)
                for c in range(TILES):
                    last = eng.tensor_scalar(mask[pair.side][:, c, :], adj_sb[pair.side][:, c, :], 0.0, None,
                                             ALU.is_gt, ALU.add, accum_out=deg[pair.side][:, c:c + 1])
                last.then_inc(masks_ready, 1)
                eng.wait_ge(masks_ready, pair.n + 1)
                eng.tensor_copy(deg16[pair.side][:, :], deg[pair.side][:, :]).then_inc(degrees_ready, 1)
                eng.tensor_tensor(key[:, :], deg[pair.side][:, :], const("tie_col"),
                                  ALU.add).then_inc(degrees_ready, 1)

            def ranks(pair):
                eng.wait_ge(keys_ready, pair.n + 1)
                for c in range(TILES):
                    g = c // NT
                    last = eng.tensor_scalar(junk[:, c, :], bx0[:, g * N:g * N + N], key[:, c:c + 1], None,
                                             ALU.is_gt, ALU.add, accum_out=rank[:, c:c + 1])
                last.then_inc(ranks_ready, 1)
                eng.wait_ge(ranks_ready, pair.n + 1)
                if pair.follows(2):
                    eng.wait_ge(permT_ready, pair.n - 1)
                for c in range(TILES):
                    last = eng.tensor_scalar(perm[pair.side][:, c, :], iota[:, :], rank[:, c:c + 1], None,
                                             ALU.is_equal)
                last.then_inc(perm_ready, 1)

            def start_sums(pair):
                eng.wait_ge(u_copied, 2 * (pair.n + 1))
                eng.wait_ge(excess_ready, pair.n + 1)
                if pair.follows(2):
                    eng.wait_ge(y_ready, pair.n - 1)
                side = pair.side
                if pair.general:
                    eng.memset(sm[side][:, :, :], 0.0).then_inc(sums_started, 2)
                    eng.memset(st[side][:, :], 0.0).then_inc(sums_started, 1)
                    return
                eng.scalar_tensor_tensor(out=sm[side][:, :, :].rearrange("p g r -> p (g r)"),
                                         in0=um[side][:, :, :].rearrange("p g r -> p (g r)"), scalar=0.0,
                                         in1=bx3[:, :], op0=ALU.max, op1=ALU.mult).then_inc(sums_started, 1)
                for g in range(2):
                    rows = slice(g * HT, g * HT + HT)
                    eng.scalar_tensor_tensor(out=st[side][rows, :], in0=ut[side][rows, :], scalar=0.0,
                                             in1=bx3[rows, g * N:g * N + N], op0=ALU.max,
                                             op1=ALU.mult).then_inc(sums_started, 1)

            def rest_v(pair, g):
                eng.wait_ge(vh_ready, 2 * pair.n + g + 1)
                if pair.follows(1):
                    eng.wait_ge(vl_ready, 2 * pair.n)
                c = slice(g * NT, g * NT + NT)
                eng.tensor_tensor(vr[:, c, :].rearrange("p t h -> p (t h)"), (bx2, bx1)[g][:, 0:NT * H],
                                  vh[pair.side][:, c, :].rearrange("p t h -> p (t h)"),
                                  ALU.subtract).then_inc(vr_ready, 1)

            def selections(pair, first, last):
                if first == 0:
                    eng.wait_ge(slots_copied, 2 * (pair.n + 1))
                    if pair.follows(2):
                        eng.wait_ge(gathered, NU * (pair.n - 1))
                side = pair.side
                for s in range(first, last):
                    c0, n = START[s], CAPS[s]
                    if s < BIG_SLOTS:
                        eng.tensor_scalar(hot[side][:, :, c0:c0 + n], slotT[:, :, 0:n], float(MARK + s), None,
                                          ALU.is_equal).then_inc(hot_ready, 1)
                    else:
                        eng.tensor_tensor(
                            hot[side][:, :, c0:].rearrange("p c (s r) -> p c s r", r=SMALL),
                            slotT[:, :, 0:SMALL].unsqueeze(2).broadcast_to([P, TILES, NSMALL, SMALL]),
                            small_marks[:, :].rearrange("p (s r) -> p s r", r=SMALL).unsqueeze(1)
                            .broadcast_to([P, TILES, NSMALL, SMALL]),
                            ALU.is_equal).then_inc(hot_ready, 1)

            def views(pair, unit, segment, b, start=0):
                tile, s0, _, _ = UNITS[unit]
                _, n = unit_cols(unit)
                first, slots = segment
                c = START[first] - START[s0]
                cap = CAPS[first]
                if tile == "main":
                    v = b[:, 0:2 * n].rearrange("p (g c) -> p g c", g=2)[:, :, c:c + slots * cap]
                    return v.rearrange("p g (s r) -> p g s r", r=cap)
                return b[:, c:c + slots * cap].rearrange("p (s r) -> p s r", r=cap)

            def shift(pair, unit):
                tile = UNITS[unit][0]
                side = pair.side
                eng.wait_ge(gathered, NU * pair.n + unit + 1)
                b, to = ring[unit % BANKS], tmp[unit % NTMP]
                for first, slots in UNITS[unit][3]:
                    cap = CAPS[first]
                    if tile == "main":
                        u = um[side][:, :, 0:cap].unsqueeze(2).broadcast_to([P, 2, slots, cap])
                    else:
                        u = ut[side][:, 0:cap].unsqueeze(1).broadcast_to([P, slots, cap])
                    eng.tensor_tensor(views(pair, unit, (first, slots), to), views(pair, unit, (first, slots), b),
                                      u, ALU.add).then_inc(shifted, 1)

            def add(pair, unit):
                tile = UNITS[unit][0]
                side = pair.side
                sums = sm[side] if tile == "main" else st[side]
                t = tmp[unit % NTMP]
                eng.wait_ge(shifted, NSHIFT * pair.n + SHIFTS_BEFORE[unit + 1])
                if unit == 0:
                    eng.wait_ge(sums_started, 3 * (pair.n + 1))
                done = ADDS_BEFORE[unit]
                for first, slots in UNITS[unit][3]:
                    cap = CAPS[first]
                    v = views(pair, unit, (first, slots), t)
                    if first < BIG_SLOTS:
                        for s in range(slots):
                            to = sums[:, :, 0:cap] if tile == "main" else sums[:, 0:cap]
                            if done or pair.follows(1):
                                eng.wait_ge(added, NADD * pair.n + done)
                            eng.scalar_tensor_tensor(out=to, in0=v[:, :, s, :] if tile == "main" else v[:, s, :],
                                                     scalar=0.0, in1=to, op0=ALU.max,
                                                     op1=ALU.add).then_inc(added, 1)
                            done += 1
                        continue
                    k = 1 if tile == "main" else 0
                    eng.tensor_scalar(v, v, 0.0, None, ALU.max).then_inc(clamped, 1)
                    eng.wait_ge(clamped, 2 * pair.n + k + 1)
                    if tile == "main":
                        part, to = small_sum[:, :, :], sums[:, :, 0:SMALL]
                        turned = v.rearrange("p g s r -> p g r s")
                    else:
                        part, to = small_sum[:, 0, :], sums[:, 0:SMALL]
                        turned = v.rearrange("p s r -> p r s")
                    eng.tensor_reduce(part, turned, AX.X, ALU.add).then_inc(reduced, 1)
                    eng.wait_ge(reduced, 2 * pair.n + k + 1)
                    if done or pair.follows(1):
                        eng.wait_ge(added, NADD * pair.n + done)
                    eng.tensor_tensor(to, to, part, ALU.add).then_inc(added, 1)
                    done += 1

            def normalise(pair):
                side = pair.side
                eng.wait_ge(z_ready, pair.n + 1)
                zf = z[:, :, :].rearrange("p t o -> p (t o)")
                eng.tensor_tensor(zf, by[:, TILES * O:2 * TILES * O],
                                  x_sb[side][:, :, :].rearrange("p t f -> p (t f)"), ALU.add).then_inc(z_added, 1)
                eng.wait_ge(z_added, pair.n + 1)
                for c in range(TILES):
                    eng.bn_stats(stats[:, c, :], z[:, c, :]).then_inc(stats_ready, 1)
                eng.wait_ge(stats_ready, TILES * (pair.n + 1))
                eng.tensor_tensor(apart[:, :], stats[:, :, 1], stats[:, :, 4], ALU.subtract).then_inc(moments_ready, 1)
                eng.tensor_tensor(within[:, :], stats[:, :, 2], stats[:, :, 5], ALU.add).then_inc(moments_ready, 1)
                eng.wait_ge(moments_ready, 5 * pair.n + 1)
                eng.scalar_tensor_tensor(out=mean[:, :], in0=apart[:, :], scalar=-0.5, in1=stats[:, :, 1],
                                         op0=ALU.mult, op1=ALU.add).then_inc(moments_ready, 1)
                eng.scalar_tensor_tensor(out=across[:, :], in0=apart[:, :], scalar=O / 4.0, in1=apart[:, :],
                                         op0=ALU.mult, op1=ALU.mult).then_inc(moments_ready, 1)
                eng.wait_ge(moments_ready, 5 * pair.n + 4)
                eng.tensor_tensor(spread[:, :], within[:, :], across[:, :], ALU.add).then_inc(moments_ready, 1)

            def scale(pair):
                side = pair.side
                eng.wait_ge(std_ready, pair.n + 1)
                eng.reciprocal(rstd[:, :], std[:, :]).then_inc(rstd_ready, 1)
                eng.wait_ge(rstd_ready, pair.n + 1)
                if pair.follows(2):
                    eng.wait_ge(stored[side], 16 * pair.half)
                for c in range(TILES):
                    last = eng.tensor_scalar(o_sb[side][:, c, :], z[:, c, :], mean[:, c:c + 1], rstd[:, c:c + 1],
                                             ALU.subtract, ALU.mult)
                last.then_inc(normed, 1)

            def prepare_all(pair):
                masks(pair)
                ranks(pair)
                start_sums(pair)
                rest_v(pair, 0)
                rest_v(pair, 1)
                if not pair.general:
                    selections(pair, 0, NHOT)

            def body(pair, prepare=True, finish=True):
                new = pair.next()
                old = pair.prev()
                shift(pair, 0)
                if prepare:
                    masks(new)
                shift(pair, 1)
                add(pair, 0)
                shift(pair, 2)
                if prepare:
                    ranks(new)
                add(pair, 1)
                shift(pair, 3)
                add(pair, 2)
                shift(pair, 4)
                add(pair, 3)
                if finish:
                    normalise(old)
                shift(pair, 5)
                add(pair, 4)
                if finish:
                    scale(old)
                shift(pair, 6)
                add(pair, 5)
                if prepare:
                    start_sums(new)
                    rest_v(new, 0)
                shift(pair, 7)
                add(pair, 6)
                if prepare:
                    rest_v(new, 1)
                    selections(new, 0, 1)
                shift(pair, 8)
                add(pair, 7)
                if prepare:
                    selections(new, 1, 3)
                shift(pair, 9)
                add(pair, 8)
                if prepare:
                    selections(new, 3, 5)
                shift(pair, 10)
                add(pair, 9)
                if prepare:
                    selections(new, 5, NHOT)
                add(pair, 10)

            prepare_all(Pair(0, 0))
            body(Pair(0, 0), finish=False)
            body(Pair(0, 1))
            with eng.Fori(1, PAIRS // 2 - 1) as i:
                body(Pair(i, 0))
                body(Pair(i, 1))
            body(Pair(0, PAIRS - 2))
            body(Pair(0, PAIRS - 1), prepare=False)
            normalise(Pair(0, PAIRS - 1))
            scale(Pair(0, PAIRS - 1))

            def general(pair):
                side = pair.side
                prepare_all(pair)
                sf = sm[side][:, :, :].rearrange("p g r -> p (g r)")
                uf = um[side][:, :, :].rearrange("p g r -> p (g r)")
                tail = tmp[1][:, 0:N]
                with eng.Fori(0, N) as s:
                    number = pair.data * N + s
                    done = number * GENERAL_STEPS
                    mark = const("marks")[:, bass.ds(s, 1)]
                    slot = const("iota")[:, bass.ds(s, 1)]
                    eng.wait_ge(slots_copied, 2 * (pair.n + 1))
                    eng.wait_ge(sums_started, 3 * (pair.n + 1))
                    eng.tensor_scalar(hot[0][:, :, 0:N], slotT[:, :, :], mark, None,
                                      ALU.is_equal).then_inc(general_hot, 1)
                    eng.wait_ge(general_gathered, number + 1)
                    eng.tensor_tensor(tmp[0][:, :], ring[0][:, :], uf, ALU.add).then_inc(general_step, 1)
                    eng.tensor_tensor(tail, ring[1][:, 0:N], ut[side][:, :], ALU.add).then_inc(general_step, 1)
                    eng.wait_ge(general_step, done + 2)
                    eng.scalar_tensor_tensor(out=tmp[0][:, :], in0=bx3[:, :], scalar=slot, in1=tmp[0][:, :],
                                             op0=ALU.is_gt, op1=ALU.mult).then_inc(general_step, 1)
                    for g in range(2):
                        rows = slice(g * HT, g * HT + HT)
                        eng.scalar_tensor_tensor(out=tail[rows, :], in0=bx3[rows, g * N:g * N + N],
                                                 scalar=slot[rows, :], in1=tail[rows, :],
                                                 op0=ALU.is_gt, op1=ALU.mult).then_inc(general_step, 1)
                    eng.wait_ge(general_step, done + 5)
                    eng.scalar_tensor_tensor(out=sf, in0=tmp[0][:, :], scalar=0.0, in1=sf,
                                             op0=ALU.max, op1=ALU.add).then_inc(general_step, 1)
                    eng.scalar_tensor_tensor(out=st[side][:, :], in0=tail, scalar=0.0, in1=st[side][:, :],
                                             op0=ALU.max, op1=ALU.add).then_inc(general_step, 1)
                    eng.wait_ge(general_step, done + GENERAL_STEPS)
                    eng.tensor_copy(idle[:, :], std[:, 0:1])
                normalise(pair)
                scale(pair)

            general_loop(eng, general)


def kernel(**inputs):
    import concourse.bacc as bacc
    from concourse.bass_utils import run_bass_kernel_spmd

    nc = bacc.Bacc("TRN2", target_bir_lowering=False, num_devices=1)
    x = np.ascontiguousarray(inputs["x"])
    arrays = {
        "x": x,
        "xT": np.ascontiguousarray(x.reshape(GRAPHS * N, F).T),
        "adj": np.ascontiguousarray(inputs["adj"]),
        "w1": np.ascontiguousarray(inputs["L0_gnn_W1"]),
        "b1": np.ascontiguousarray(inputs["L0_gnn_b1"]),
        "w2": np.ascontiguousarray(inputs["L0_gnn_W2"]),
        "b2": np.ascontiguousarray(inputs["L0_gnn_b2"]),
        "consts": constants(),
    }
    args = [nc.dram_tensor(name, a.shape, mybir.dt.from_np(a.dtype), kind="ExternalInput").ap()
            for name, a in arrays.items()]
    out = nc.dram_tensor("out", (GRAPHS, N, F), F32, kind="ExternalOutput").ap()
    build(nc, *args, out)
    return run_bass_kernel_spmd(nc, [arrays], core_ids=[0]).results[0]["out"]
```

```python
from contextlib import ExitStack

import numpy as np

import concourse.bass as bass
from concourse import mybir

ALU = mybir.AluOpType
ACT = mybir.ActivationFunctionType
F32 = mybir.dt.float32
BF16 = mybir.dt.bfloat16
F16 = mybir.dt.float16
I32 = mybir.dt.int32
AX = mybir.AxisListType

GRAPHS, N, F, H, O = 32, 256, 64, 192, 64
EPS = 1e-5
P = 128
NT = N // P
PAIRS = GRAPHS // 2
HT = H - P
TILES = 2 * NT
X_CHUNKS = 4
TOP = 13
LEAST_BOUND = 2.0 ** -80
EXPONENT = 0x7F800000
BIAS, MANTISSA = 127, 23
MARK = 2 * N

SMALL, NSMALL = 16, 8
CAPS = [256, 256, 256, 224, 184, 128, 88, 48, 48] + [SMALL] * NSMALL
START = [sum(CAPS[:s]) for s in range(len(CAPS))]
COLS = sum(CAPS)
BIG_SLOTS = len(CAPS) - NSMALL


def slots_given(rank):
    return sum(c > rank for c in CAPS)


UNITS = [
    ("main", 0, 1, [(0, 1)]),
    ("tail", 0, 2, [(0, 2)]),
    ("main", 1, 2, [(1, 1)]),
    ("tail", 2, 4, [(2, 1), (3, 1)]),
    ("main", 2, 3, [(2, 1)]),
    ("tail", 4, 7, [(4, 1), (5, 1), (6, 1)]),
    ("main", 3, 4, [(3, 1)]),
    ("main", 4, 5, [(4, 1)]),
    ("tail", 7, 17, [(7, 2), (9, 8)]),
    ("main", 5, 7, [(5, 1), (6, 1)]),
    ("main", 7, 17, [(7, 2), (9, 8)]),
]
NU = len(UNITS)
BANKS = 3


def unit_cols(unit):
    _, s0, s1, _ = UNITS[unit]
    return START[s0], sum(CAPS[s0:s1])


def adds_of(unit):
    return sum(1 if s0 >= BIG_SLOTS else n for s0, n in UNITS[unit][3])


SHIFTS = [len(u[3]) for u in UNITS]
SHIFTS_BEFORE = [sum(SHIFTS[:u]) for u in range(NU + 1)]
ADDS_BEFORE = [sum(adds_of(i) for i in range(u)) for u in range(NU + 1)]
NSHIFT, NADD = SHIFTS_BEFORE[NU], ADDS_BEFORE[NU]
NHOT = BIG_SLOTS + 1

GENERAL_STEPS = 7

CONSTS = {}


def constants():
    p = np.arange(P)[:, None]
    node = np.arange(TILES * P)[None, :] % N
    parts = dict(
        ident=np.eye(P),
        iota=np.broadcast_to(np.arange(N)[None, :], (P, N)),
        signs=np.broadcast_to(2 * np.arange(N)[None, :] - (N - 1), (P, N)),
        tie_row=np.broadcast_to((N - 1 - node) / N, (P, 2 * N)),
        neg_tie_col=-(N - 1 - (np.arange(TILES)[None, :] % NT * P + p)) / N,
        neg_given=np.broadcast_to([-slots_given(r) for r in range(N)] * 2, (P, 2 * N)),
        before=(p < np.arange(P)[None, :]) + MARK * np.eye(P),
        small_marks=np.broadcast_to(
            np.repeat(MARK + BIG_SLOTS + np.arange(NSMALL), SMALL)[None, :], (P, NSMALL * SMALL)),
        marks=np.broadcast_to(MARK + np.arange(N)[None, :], (P, N)),
        eps=np.full((P, 1), EPS),
    )
    at = 0
    for name, a in parts.items():
        CONSTS[name] = (at, a.shape[1])
        at += a.shape[1]
    return np.ascontiguousarray(np.concatenate(list(parts.values()), axis=1).astype(np.float32))


class Pair:

    def __init__(self, i, offset, general=False):
        base = PAIRS if general else 0
        self.n = 2 * i + (offset + base)
        self.half = i + (offset + base) // 2
        self.side = offset % 2
        self.data = 2 * i + offset
        self.general = general
        self.i, self.offset = i, offset

    def follows(self, k):
        return not isinstance(self.n, int) or self.n >= k

    def at(self, distance):
        return Pair(self.i, self.offset + distance, self.general)


def build(nc, x, xT, adj, w1, b1, w2, b2, consts, out):
    x_v = x.rearrange("(g two) (t p) f -> g p (two t) f", two=2, p=P)
    adj_v = adj.rearrange("(g two) (t p) k -> g p (two t) k", two=2, p=P)
    out_v = out.rearrange("(g two) (t p) f -> g p (two t) f", two=2, p=P)
    xT_v = xT.rearrange("f (g n) -> g f n", n=2 * N)

    with ExitStack() as ctx:
        def sb(name, shape, dt=F32):
            return ctx.enter_context(nc.sbuf_tensor(name, shape, dt))

        def bank(name):
            return ctx.enter_context(nc.psum_tensor(name, [P, 512], F32))

        def sem(name):
            return ctx.enter_context(nc.semaphore(name))

        def both(name, shape, dt=F32):
            return [sb(f"{name}{s}", shape, dt) for s in range(2)]

        cst = sb("cst", [P, consts.shape[1]])

        def const(name):
            at, n = CONSTS[name]
            return cst[:, at:at + n]

        ident = sb("ident", [P, P], BF16)
        signs = sb("signs", [P, N], BF16)
        tie_row = sb("tie_row", [P, 2 * N], BF16)
        neg_given = sb("neg_given", [P, 2 * N], BF16)
        before = sb("before", [P, P], BF16)
        ones = sb("ones", [P, P], BF16)
        small_marks = sb("small_marks", [P, NSMALL * SMALL], F16)
        w1a = sb("w1a", [F, H])
        w1b = sb("w1b", [F, H])
        w1ab = sb("w1ab", [F, H])
        w1n = sb("w1n", [F, H])
        b1m = sb("b1m", [P, 1])
        b1t = sb("b1t", [P, 1])
        w2m = sb("w2m", [P, O])
        w2t = sb("w2t", [P, 2, O])
        b2b = sb("b2b", [P, O])
        ones32 = sb("ones32", [P, P])
        x_all = sb("x_all", [P, X_CHUNKS, GRAPHS * N * F // P // X_CHUNKS])
        x_max = sb("x_max", [P, X_CHUNKS])
        x_max1 = sb("x_max1", [P, 1])
        x_top = sb("x_top", [1, 1])
        w_abs = sb("w_abs", [F, H])
        w_top = sb("w_top", [P, 1])
        bound = sb("bound", [P, 1])
        bound1 = sb("bound1", [P, 1])
        power = sb("power", [P, 1], I32)
        up_bits = sb("up_bits", [P, 1], I32)
        down = sb("down", [P, 1])
        w1s = sb("w1s", [F, H])
        b1ms, b1ts = sb("b1ms", [P, 1]), sb("b1ts", [P, 1])
        w2ms, w2ts = sb("w2ms", [P, O]), sb("w2ts", [P, 2, O])
        adj_sb = both("adj_sb", [P, TILES, N])
        x_sb = both("x_sb", [P, TILES, F])
        xT_sb = both("xT_sb", [F, 2 * N])
        mask = both("mask", [P, TILES, N], BF16)
        deg = both("deg", [P, TILES])
        deg16 = both("deg16", [P, TILES], BF16)
        neg_key = sb("neg_key", [P, TILES])
        rank = sb("rank", [P, TILES])
        junk = sb("junk", [P, TILES, N], BF16)
        junk2 = sb("junk2", [P, TILES, N], BF16)
        perm = both("perm", [P, TILES, N], BF16)
        permT = sb("permT", [P, TILES, N])
        maskT = sb("maskT", [P, TILES, N], BF16)
        slotT = sb("slotT", [P, TILES, N], F16)
        hot = both("hot", [P, TILES, COLS], BF16)
        excess_junk = sb("excess_junk", [1, 2 * N])
        over = sb("over", [1, 1])
        over_sum = sb("over_sum", [1, 1])
        over_int = sb("over_int", [1, 1], I32)
        xb = both("xb", [P, TILES, F])
        db = sb("db", [P, TILES, F])
        xh = sb("xh", [P, TILES, F], BF16)
        xm = sb("xm", [P, TILES, F], BF16)
        xl = sb("xl", [P, TILES, F], BF16)
        xr = sb("xr", [P, TILES, F])
        xs = sb("xs", [F, 2 * N])
        vh = both("vh", [P, TILES, H], F16)
        vl = both("vl", [P, TILES, H], F16)
        um = both("um", [P, 2, N])
        ut = both("ut", [P, N])
        sm = both("sm", [P, 2, N])
        st = both("st", [P, N])
        NTMP = 3
        tmp = [sb(f"tmp{i}", [P, 512]) for i in range(NTMP)]
        small_sum, small_sum_t = sb("small_sum", [P, 2, SMALL]), sb("small_sum_t", [P, SMALL])
        vf = sb("vf", [P, TILES, H])
        y_sb = sb("y_sb", [P, TILES, O])
        z = sb("z", [P, TILES, O])
        stats = sb("stats", [P, TILES, 6])
        apart, within, across = sb("apart", [P, TILES]), sb("within", [P, TILES]), sb("across", [P, TILES])
        mean = sb("mean", [P, TILES])
        spread = sb("spread", [P, TILES])
        std = sb("std", [P, TILES])
        rstd = sb("rstd", [P, TILES])
        centred = sb("centred", [P, TILES, O])
        idle = sb("idle", [P, 1])
        o_sb = both("o_sb", [P, TILES, O])

        bx0, bx1, bx2, bx3 = (bank(f"bx{i}") for i in range(4))
        by = bank("by")
        ring = [bank(f"ring{i}") for i in range(BANKS)]

        consts_loaded, weights_loaded = sem("consts_loaded"), sem("weights_loaded")
        consts_ready, weights_ready = sem("consts_ready"), sem("weights_ready")
        x_all_loaded = [sem(f"x_all_loaded{c}") for c in range(X_CHUNKS)]
        scale_step = sem("scale_step")
        w_sums_ready, x_turned, x_top_spread = sem("w_sums_ready"), sem("x_turned"), sem("x_top_spread")
        adj_loaded = [sem(f"adj_loaded{s}") for s in range(2)]
        x_loaded = [sem(f"x_loaded{s}") for s in range(2)]
        xT_loaded = [sem(f"xT_loaded{s}") for s in range(2)]
        stored = [sem(f"stored{s}") for s in range(2)]
        masks_ready = sem("masks_ready")
        degrees_ready = sem("degrees_ready")
        degrees_copied = sem("degrees_copied")
        keys_ready = sem("keys_ready")
        ranks_ready = sem("ranks_ready")
        perm_ready = sem("perm_ready")
        maskT_ready = sem("maskT_ready")
        maskT_copied = sem("maskT_copied")
        slots_ready = sem("slots_ready")
        slots_copied = sem("slots_copied")
        excess_ready = sem("excess_ready")
        over_ready = sem("over_ready")
        over_added = sem("over_added")
        db_ready, xb_ready = sem("db_ready"), sem("xb_ready")
        xh_ready, xr_ready = sem("xh_ready"), sem("xr_ready")
        xm_ready, xl_ready = sem("xm_ready"), sem("xl_ready")
        xs_ready, xs_copied = sem("xs_ready"), sem("xs_copied")
        u_ready, u_copied = sem("u_ready"), sem("u_copied")
        v_ready, vh_ready = sem("v_ready"), sem("vh_ready")
        vf_ready, vl_ready = sem("vf_ready"), sem("vl_ready")
        sums_started = sem("sums_started")
        hot_ready = sem("hot_ready")
        gathered = sem("gathered")
        shifted = sem("shifted")
        clamped, reduced = sem("clamped"), sem("reduced")
        added = sem("added")
        permT_ready, permT_copied = sem("permT_ready"), sem("permT_copied")
        y_ready, y_copied = sem("y_ready"), sem("y_copied")
        z_ready, z_added = sem("z_ready"), sem("z_added")
        stats_ready, moments_ready = sem("stats_ready"), sem("moments_ready")
        std_ready, rstd_ready = sem("std_ready"), sem("rstd_ready")
        mean_ready, centred_ready = sem("mean_ready"), sem("centred_ready")
        normed = sem("normed")
        over_all = sem("over_all")
        general_hot, general_gathered = sem("general_hot"), sem("general_gathered")
        general_step = sem("general_step")

        block = ctx.enter_context(nc.Block())

        def general_loop(eng, body, after=None):
            eng.wait_ge(over_all, 1)
            needed = eng.value_load(over_int[0:1, 0:1], min_val=0, max_val=GRAPHS * N * N)
            with eng.If(needed > 0):
                with eng.Fori(0, PAIRS // 2) as i:
                    for side in range(2):
                        pair = Pair(i, side, general=True)
                        eng.wait_ge(normed, pair.n)
                        body(pair)
                if after:
                    after()

        @block.sync
        def _(eng):
            eng.dma_start(cst[:, :], consts[:, :]).then_inc(consts_loaded, 16)

            def load_adj(pair):
                if not pair.general and pair.follows(2):
                    eng.wait_ge(masks_ready, pair.n - 1)
                eng.dma_start(adj_sb[pair.side][:, :, :], adj_v[pair.data]).then_inc(adj_loaded[pair.side], 16)

            def load_xT(pair):
                if not pair.general and pair.follows(2):
                    eng.wait_ge(v_ready, 2 * (pair.n - 1))
                eng.dma_start(xT_sb[pair.side][:, :], xT_v[pair.data]).then_inc(xT_loaded[pair.side], 16)

            def load_x(pair):
                if not pair.general and pair.follows(2):
                    eng.wait_ge(xb_ready, pair.n - 1)
                eng.dma_start(x_sb[pair.side][:, :, :], x_v[pair.data]).then_inc(x_loaded[pair.side], 16)

            def store(pair):
                eng.wait_ge(normed, pair.n + 1)
                eng.dma_start(out_v[pair.data], o_sb[pair.side][:, :, :]).then_inc(stored[pair.side], 16)

            def body(pair, first=False):
                load_adj(pair)
                load_xT(pair.at(-1))
                load_x(pair)
                if not first:
                    store(pair.at(-4))

            load_adj(Pair(0, 0))
            load_x(Pair(0, 0))
            eng.dma_start(w1a[:, :], w1[0:F, :]).then_inc(weights_loaded, 16)
            eng.dma_start(w1b[:, :], w1[F:2 * F, :]).then_inc(weights_loaded, 16)
            for half in range(2):
                rows = slice(half * HT, half * HT + HT)
                eng.dma_start(b1t[rows, :], b1[P:H].rearrange("(h one) -> h one", one=1)).then_inc(weights_loaded, 16)
                eng.dma_start(w2t[rows, half, :], w2[P:H, :]).then_inc(weights_loaded, 16)
            eng.dma_start(b1m[:, :], b1[0:P].rearrange("(h one) -> h one", one=1)).then_inc(weights_loaded, 16)
            eng.dma_start(w2m[:, :], w2[0:P, :]).then_inc(weights_loaded, 16)
            eng.dma_start(b2b[:, :], b2.rearrange("(one o) -> one o", one=1).broadcast_to([P, O])
                          ).then_inc(weights_loaded, 16)
            x_all_v = x.rearrange("g n f -> (g n f)").rearrange("(p c m) -> p c m", p=P, c=X_CHUNKS)
            for c in range(X_CHUNKS):
                eng.dma_start(x_all[:, c, :], x_all_v[:, c, :]).then_inc(x_all_loaded[c], 16)
            load_adj(Pair(0, 1))
            load_x(Pair(0, 1))
            load_xT(Pair(0, 0))
            load_adj(Pair(0, 2))
            load_xT(Pair(0, 1))
            load_x(Pair(0, 2))
            body(Pair(0, 3), first=True)
            with eng.Fori(2, PAIRS // 2) as i:
                body(Pair(i, 0))
                body(Pair(i, 1))
            load_xT(Pair(0, PAIRS - 1))
            for left in range(4, 0, -1):
                store(Pair(0, PAIRS - left))
            for side in range(2):
                eng.wait_ge(stored[side], 16 * (PAIRS // 2))

            def general(pair):
                load_adj(pair)
                load_xT(pair)
                load_x(pair)
                store(pair)

            def all_stored():
                for side in range(2):
                    eng.wait_ge(stored[side], 16 * PAIRS)

            general_loop(eng, general, all_stored)

        @block.gpsimd
        def _(eng):
            def split_x(pair):
                eng.wait_ge(xh_ready, pair.n + 1)
                if pair.follows(1):
                    eng.wait_ge(xm_ready, pair.n)
                eng.tensor_tensor(xr[:, :, :], x_sb[pair.side][:, :, :], xh[:, :, :],
                                  ALU.subtract).then_inc(xr_ready, 1)
                eng.wait_ge(xm_ready, pair.n + 1)
                eng.wait_ge(xr_ready, pair.n + 1)
                eng.tensor_tensor(xl[:, :, :], xr[:, :, :], xm[:, :, :], ALU.subtract).then_inc(xl_ready, 1)

            def residual(pair):
                eng.wait_ge(degrees_ready, TILES * (pair.n + 1))
                eng.tensor_tensor(db[:, :, :], deg[pair.side][:, :].unsqueeze(2).broadcast_to([P, TILES, F]),
                                  b2b[:, :].unsqueeze(1).broadcast_to([P, TILES, F]), ALU.mult).then_inc(db_ready, 1)
                eng.wait_ge(db_ready, pair.n + 1)
                if pair.follows(2):
                    eng.wait_ge(z_added, pair.n - 1)
                eng.tensor_tensor(xb[pair.side][:, :, :], db[:, :, :], x_sb[pair.side][:, :, :],
                                  ALU.add).then_inc(xb_ready, 1)

            def low_v(pair, g):
                eng.wait_ge(vf_ready, 2 * pair.n + g + 1)
                if not pair.general and pair.follows(2):
                    eng.wait_ge(gathered, NU * (pair.n - 1))
                c = slice(g * NT, g * NT + NT)
                eng.tensor_tensor(vl[pair.side][:, c, :], vf[:, c, :], vh[pair.side][:, c, :],
                                  ALU.subtract).then_inc(vl_ready, 1)

            def count_over(pair):
                eng.wait_ge(over_ready, pair.n + 1)
                eng.wait_ge(over_added, pair.n + 1)
                eng.tensor_tensor(over_sum[:, :], over_sum[:, :], over[:, :], ALU.add).then_inc(over_added, 1)

            def scale(pair):
                eng.wait_ge(mean_ready, pair.n + 1)
                if pair.follows(1):
                    eng.wait_ge(normed, pair.n)
                eng.tensor_tensor(centred[:, :, :], z[:, :, :],
                                  mean[:, :].unsqueeze(2).broadcast_to([P, TILES, O]), ALU.subtract
                                  ).then_inc(centred_ready, 1)
                eng.wait_ge(rstd_ready, pair.n + 1)
                eng.wait_ge(centred_ready, pair.n + 1)
                if pair.follows(2):
                    eng.wait_ge(stored[pair.side], 16 * pair.half)
                eng.tensor_tensor(o_sb[pair.side][:, :, :], centred[:, :, :],
                                  rstd[:, :].unsqueeze(2).broadcast_to([P, TILES, O]), ALU.mult).then_inc(normed, 1)

            def body(pair, order=True, prepare=True, finish=True):
                if prepare:
                    residual(pair.at(1))
                if finish:
                    scale(pair.at(-1))
                if prepare and not pair.general:
                    count_over(pair.at(1))
                if prepare:
                    low_v(pair.at(1), 0)
                    low_v(pair.at(1), 1)
                if order:
                    split_x(pair.at(2))

            eng.wait_ge(weights_loaded, 16 * 9)
            body(Pair(0, -2), prepare=False, finish=False)
            body(Pair(0, -1), finish=False)
            body(Pair(0, 0), finish=False)
            body(Pair(0, 1))
            with eng.Fori(1, PAIRS // 2 - 1) as i:
                body(Pair(i, 0))
                body(Pair(i, 1))
            body(Pair(0, PAIRS - 2), order=False)
            body(Pair(0, PAIRS - 1), order=False, prepare=False)
            body(Pair(0, PAIRS), order=False, prepare=False)
            eng.wait_ge(over_added, PAIRS + 1)
            eng.tensor_copy(over_int[:, :], over_sum[:, :]).then_inc(over_all, 1)

            def general(pair):
                body(pair.at(-2), prepare=False, finish=False)
                body(pair.at(-1), order=False, finish=False)
                body(pair.at(1), order=False, prepare=False)

            general_loop(eng, general)

        @block.scalar
        def _(eng):
            eng.wait_ge(consts_loaded, 16)
            for to, name in ((ident, "ident"), (signs, "signs"), (tie_row, "tie_row"), (neg_given, "neg_given"),
                             (before, "before"), (small_marks, "small_marks")):
                eng.copy(to[:, :], const(name)).then_inc(consts_ready, 1)

            def degrees(pair):
                eng.wait_ge(masks_ready, pair.n + 1)
                if pair.follows(2):
                    eng.wait_ge(xb_ready, pair.n - 1)
                for c in range(TILES):
                    eng.activation(junk[:, c, :], mask[pair.side][:, c, :], ACT.Copy,
                                   accum_out=deg[pair.side][:, c:c + 1]).then_inc(degrees_ready, 1)

            def ranks(pair):
                eng.wait_ge(keys_ready, pair.n + 1)
                if pair.follows(1):
                    eng.wait_ge(perm_ready, pair.n)
                for c in range(TILES):
                    g = c // NT
                    last = eng.activation(junk2[:, c, :], bx0[:, g * N:g * N + N], ACT.Sign,
                                          bias=neg_key[:, c:c + 1], accum_out=rank[:, c:c + 1])
                last.then_inc(ranks_ready, 1)

            def high_x(pair):
                eng.wait_ge(x_loaded[pair.side], 16 * (pair.half + 1))
                if pair.follows(1):
                    eng.wait_ge(xs_ready, pair.n)
                eng.copy(xh[:, :, :], x_sb[pair.side][:, :, :]).then_inc(xh_ready, 1)

            def middle_x(pair):
                eng.wait_ge(xr_ready, pair.n + 1)
                eng.copy(xm[:, :, :], xr[:, :, :]).then_inc(xm_ready, 1)

            def copy_maskT(pair):
                for g, b in enumerate((bx1, bx2)):
                    eng.wait_ge(maskT_ready, 2 * pair.n + g + 1)
                    if pair.follows(1):
                        eng.wait_ge(slots_ready, 2 * (pair.n - 1) + g + 1)
                    eng.copy(maskT[:, g * NT:g * NT + NT, :].rearrange("p t r -> p (t r)"),
                             b[:, :]).then_inc(maskT_copied, 1)

            def copy_slots(pair):
                if not pair.general and pair.follows(1):
                    eng.wait_ge(hot_ready, NHOT * pair.n)
                for g, b in enumerate((bx0, bx1)):
                    eng.wait_ge(slots_ready, 2 * pair.n + g + 1)
                    eng.copy(slotT[:, g * NT:g * NT + NT, :].rearrange("p t r -> p (t r)"),
                             b[:, :]).then_inc(slots_copied, 1)

            def look_over(pair):
                eng.wait_ge(excess_ready, pair.n + 1)
                eng.wait_ge(over_added, pair.n + 1)
                eng.activation(excess_junk[:, :], bx3[0:1, :], ACT.Relu, accum_out=over[:, :]).then_inc(over_ready, 1)

            def copy_xs(pair):
                eng.wait_ge(xs_ready, pair.n + 1)
                if pair.follows(1):
                    eng.wait_ge(u_ready, 2 * pair.n)
                eng.copy(xs[:, :], bx2[0:F, :]).then_inc(xs_copied, 1)

            def copy_u(pair):
                if not pair.general and pair.follows(2):
                    eng.wait_ge(shifted, NSHIFT * (pair.n - 1))
                eng.wait_ge(u_ready, 2 * pair.n + 1)
                eng.activation(um[pair.side][:, :, :].rearrange("p g r -> p (g r)"), bx0[:, :], ACT.Identity,
                               bias=b1ms[:, 0:1]).then_inc(u_copied, 1)
                eng.wait_ge(u_ready, 2 * pair.n + 2)
                eng.activation(ut[pair.side][:, :], bx1[:, 0:N], ACT.Identity,
                               bias=b1ts[:, 0:1]).then_inc(u_copied, 1)

            def high_v(pair, g):
                eng.wait_ge(v_ready, 2 * pair.n + g + 1)
                if not pair.general and pair.follows(2):
                    eng.wait_ge(gathered, NU * (pair.n - 1))
                b = (bx2, bx1)[g]
                eng.copy(vh[pair.side][:, g * NT:g * NT + NT, :].rearrange("p t h -> p (t h)"),
                         b[:, 0:NT * H]).then_inc(vh_ready, 1)
                if pair.follows(1):
                    eng.wait_ge(vl_ready, 2 * (pair.n - 1) + g + 1)
                eng.copy(vf[:, g * NT:g * NT + NT, :].rearrange("p t h -> p (t h)"),
                         b[:, 0:NT * H]).then_inc(vf_ready, 1)

            def copy_permT(pair):
                eng.wait_ge(permT_ready, pair.n + 1)
                if pair.follows(1):
                    eng.wait_ge(z_ready, pair.n)
                eng.copy(permT[:, :, :].rearrange("p t n -> p (t n)"), bx3[:, :].bitcast(BF16)).then_inc(permT_copied, 1)

            def copy_y(pair):
                eng.wait_ge(y_ready, pair.n + 1)
                if pair.follows(1):
                    eng.wait_ge(z_ready, pair.n)
                eng.copy(y_sb[:, :, :].rearrange("p t o -> p (t o)"), by[:, 0:TILES * O]).then_inc(y_copied, 1)

            def deviation(pair):
                eng.wait_ge(moments_ready, 4 * (pair.n + 1))
                if pair.follows(1):
                    eng.wait_ge(rstd_ready, pair.n)
                eng.activation(std[:, :], spread[:, :], ACT.Sqrt, scale=1.0 / O,
                               bias=const("eps")).then_inc(std_ready, 1)

            def body(pair, order=True, prepare=True, turn=True, finish=True):
                new, old, second = pair.at(1), pair.at(-1), pair.at(2)
                if prepare:
                    copy_maskT(new)
                    if not pair.general:
                        look_over(new)
                    copy_slots(new)
                if finish:
                    copy_y(old)
                if order:
                    degrees(second)
                if prepare:
                    copy_xs(new)
                    copy_u(new)
                if finish:
                    deviation(old)
                if prepare:
                    high_v(new, 0)
                    high_v(new, 1)
                if order:
                    high_x(second)
                    ranks(second)
                    middle_x(second)
                if turn:
                    copy_permT(pair)

            body(Pair(0, -2), prepare=False, turn=False, finish=False)
            body(Pair(0, -1), turn=False, finish=False)
            body(Pair(0, 0), finish=False)
            body(Pair(0, 1))
            with eng.Fori(1, PAIRS // 2 - 1) as i:
                body(Pair(i, 0))
                body(Pair(i, 1))
            body(Pair(0, PAIRS - 2), order=False)
            body(Pair(0, PAIRS - 1), order=False, prepare=False)
            body(Pair(0, PAIRS), order=False, prepare=False, turn=False)

            def general(pair):
                body(pair.at(-2), prepare=False, turn=False, finish=False)
                body(pair.at(-1), order=False, turn=False, finish=False)
                body(pair, order=False, prepare=False, finish=False)
                body(pair.at(1), order=False, prepare=False, turn=False)

            general_loop(eng, general)

        @block.tensor
        def _(eng):
            eng.wait_ge(consts_ready, 7)
            def spread_bounds():
                eng.wait_ge(scale_step, X_CHUNKS + 1)
                eng.matmul(ring[0][:, 0:H], ones32[0:F, :], w_abs[:, :], start=True, stop=True).then_inc(w_sums_ready, 1)
                eng.wait_ge(scale_step, X_CHUNKS + 2)
                eng.matmul(ring[1][0:1, 0:P], x_max1[:, :], const("ident"), start=True, stop=True).then_inc(x_turned, 1)
                eng.wait_ge(scale_step, X_CHUNKS + 4)
                eng.matmul(ring[2][:, 0:1], ones32[0:1, :], x_top[:, :], start=True, stop=True).then_inc(x_top_spread, 1)

            def keys(pair):
                eng.wait_ge(degrees_copied, 2 * (pair.n + 1))
                if pair.follows(1):
                    eng.wait_ge(u_copied, 2 * pair.n)
                for c in range(TILES):
                    eng.matmul(bx0[:, c * P:c * P + P], deg16[pair.side][:, c:c + 1].to_broadcast([P, P]),
                               ident[:, :], start=True, stop=False)
                    last = eng.matmul(bx0[:, c * P:c * P + P], ones[0:1, :], tie_row[0:1, c * P:c * P + P],
                                      start=False, stop=True)
                last.then_inc(keys_ready, 1)

            def turn_masks(pair):
                eng.wait_ge(perm_ready, pair.n + 1)
                if pair.follows(1):
                    eng.wait_ge(vf_ready, 2 * pair.n)
                for g, b in enumerate((bx1, bx2)):
                    for k in range(NT):
                        for t in range(NT):
                            last = eng.matmul(b[:, k * N:k * N + N], mask[pair.side][:, g * NT + t, k * P:k * P + P],
                                              perm[pair.side][:, g * NT + t, :], start=(t == 0), stop=(t == NT - 1))
                    last.then_inc(maskT_ready, 1)

            def excesses(pair):
                if pair.general:
                    eng.wait_ge(permT_copied, pair.n)
                elif pair.follows(2):
                    eng.wait_ge(permT_copied, pair.n - 1)
                for g in range(2):
                    for t in range(NT):
                        last = eng.matmul(bx3[:, g * N:g * N + N],
                                          deg16[pair.side][:, g * NT + t:g * NT + t + 1].to_broadcast([P, P]),
                                          perm[pair.side][:, g * NT + t, :], start=(t == 0),
                                          stop=(pair.general and t == NT - 1))
                    if not pair.general:
                        last = eng.matmul(bx3[:, g * N:g * N + N], ones[0:1, :], neg_given[0:1, g * N:g * N + N],
                                          start=False, stop=True)
                last.then_inc(excess_ready, 1)

            def number_slots(pair):
                for g, b in enumerate((bx0, bx1)):
                    eng.wait_ge(maskT_copied, 2 * pair.n + g + 1)
                    eng.matmul(b[:, 0:N], before[:, :], maskT[:, g * NT, :], start=True, stop=True)
                    eng.matmul(b[:, N:2 * N], ones[:, :], maskT[:, g * NT, :], start=True, stop=False)
                    eng.matmul(b[:, N:2 * N], before[:, :], maskT[:, g * NT + 1, :], start=False,
                               stop=True).then_inc(slots_ready, 1)

            def sort_x(pair):
                eng.wait_ge(xl_ready, pair.n + 1)
                eng.wait_ge(maskT_copied, 2 * pair.n + 2)
                steps = [(t, part) for t in range(NT) for part in (xh, xm, xl)]
                for g in range(2):
                    for s, (t, part) in enumerate(steps):
                        last = eng.matmul(bx2[0:F, g * N:g * N + N], part[:, g * NT + t, :],
                                          perm[pair.side][:, g * NT + t, :], start=(s == 0),
                                          stop=(s == len(steps) - 1))
                last.then_inc(xs_ready, 1)

            def hidden_u(pair):
                if not pair.follows(1):
                    eng.wait_ge(weights_ready, 9)
                eng.wait_ge(xs_copied, pair.n + 1)
                eng.wait_ge(slots_copied, 2 * pair.n + 2)
                eng.matmul(bx0[:, :], w1ab[:, 0:P], xs[:, :], start=True, stop=True).then_inc(u_ready, 1)
                for g in range(2):
                    last = eng.matmul(bx1[g * HT:g * HT + HT, 0:N], w1ab[:, P:H], xs[:, g * N:g * N + N],
                                      start=True, stop=True, skip_group_check=True)
                last.then_inc(u_ready, 1)

            def hidden_v(pair, g):
                eng.wait_ge(xT_loaded[pair.side], 16 * (pair.half + 1))
                if g == 1:
                    eng.wait_ge(u_copied, 2 * (pair.n + 1))
                b = (bx2, bx1)[g]
                for t in range(NT):
                    last = eng.matmul(b[:, t * H:t * H + H], xT_sb[pair.side][:, (g * NT + t) * P:(g * NT + t + 1) * P],
                                      w1n[0:F, :], start=True, stop=True)
                last.then_inc(v_ready, 1)

            def turn_perm(pair, next_started=True):
                eng.wait_ge(perm_ready, pair.n + 1)
                eng.wait_ge(sums_started, 3 * (pair.n + (2 if next_started else 1)))
                if not pair.general:
                    eng.wait_ge(over_ready, pair.n + (2 if next_started else 1))
                to = bx3[:, :].bitcast(BF16)
                for g in range(2):
                    for r in range(NT):
                        for t in range(NT):
                            at = (g * NT + r) * N + t * P
                            last = eng.transpose(to[:, at:at + P], perm[pair.side][:, g * NT + t, r * P:r * P + P],
                                                 ident[:, :])
                last.then_inc(permT_ready, 1)

            def project(pair):
                if pair.general:
                    eng.wait_ge(general_step, (pair.data + 1) * (N * GENERAL_STEPS))
                else:
                    eng.wait_ge(added, NADD * (pair.n + 1))
                if pair.follows(1):
                    eng.wait_ge(z_added, pair.n)
                for g in range(2):
                    for r in range(NT):
                        to = by[:, (g * NT + r) * O:(g * NT + r + 1) * O]
                        cols = slice(r * P, r * P + P)
                        eng.matmul(to, sm[pair.side][:, g, cols], w2ms[:, :], start=True, stop=False)
                        last = eng.matmul(to, st[pair.side][:, cols], w2ts[:, g, :], start=False, stop=True)
                last.then_inc(y_ready, 1)

            def unsort_y(pair):
                eng.wait_ge(y_copied, pair.n + 1)
                eng.wait_ge(permT_copied, pair.n + 1)
                for g in range(2):
                    for t in range(NT):
                        at = TILES * O + (g * NT + t) * O
                        for r in range(NT):
                            last = eng.matmul(by[:, at:at + O], permT[:, g * NT + r, t * P:t * P + P],
                                              y_sb[:, g * NT + r, :], start=(r == 0), stop=(r == NT - 1))
                last.then_inc(z_ready, 1)

            def gather_into(side, b, tile, selection, n):
                steps = [(k, part) for k in range(NT) for part in (vh, vl)]
                if tile == "main":
                    for g in range(2):
                        for s, (k, part) in enumerate(steps):
                            last = eng.matmul(b[:, g * n:g * n + n], part[side][:, g * NT + k, 0:P],
                                              selection(g * NT + k), start=(s == 0), stop=(s == len(steps) - 1))
                else:
                    for s, (k, part) in enumerate(steps):
                        for g in range(2):
                            last = eng.matmul(b[g * HT:g * HT + HT, 0:n], part[side][:, g * NT + k, P:H],
                                              selection(g * NT + k), start=(s == 0), stop=(s == len(steps) - 1),
                                              skip_group_check=True)
                return last

            def gather(pair, unit):
                tile, s0, s1, _ = UNITS[unit]
                c0, n = unit_cols(unit)
                if unit == 0:
                    eng.wait_ge(vl_ready, 2 * (pair.n + 1))
                eng.wait_ge(hot_ready, NHOT * pair.n + min(s1, NHOT))
                if unit >= BANKS:
                    eng.wait_ge(shifted, NSHIFT * pair.n + SHIFTS_BEFORE[unit - BANKS + 1])
                else:
                    before_it = max(u for u in range(NU) if u % BANKS == unit)
                    if pair.follows(1):
                        eng.wait_ge(shifted, NSHIFT * (pair.n - 1) + SHIFTS_BEFORE[before_it + 1])
                b = ring[unit % BANKS]
                gather_into(pair.side, b, tile, lambda c: hot[pair.side][:, c, c0:c0 + n], n).then_inc(gathered, 1)

            def prepare_all(pair):
                turn_masks(pair)
                excesses(pair)
                number_slots(pair)
                sort_x(pair)
                if not pair.follows(1):
                    spread_bounds()
                hidden_u(pair)
                hidden_v(pair, 0)
                hidden_v(pair, 1)

            def body(pair, order=True, prepare=True, finish=True):
                new, old, second = pair.at(1), pair.at(-1), pair.at(2)
                gather(pair, 0)
                if prepare:
                    turn_masks(new)
                gather(pair, 1)
                if prepare:
                    excesses(new)
                gather(pair, 2)
                if prepare:
                    number_slots(new)
                if finish:
                    project(old)
                gather(pair, 3)
                if prepare:
                    sort_x(new)
                gather(pair, 4)
                if finish:
                    unsort_y(old)
                gather(pair, 5)
                if prepare:
                    hidden_u(new)
                gather(pair, 6)
                if prepare:
                    hidden_v(new, 0)
                gather(pair, 7)
                if prepare:
                    hidden_v(new, 1)
                if order:
                    keys(second)
                gather(pair, 8)
                gather(pair, 9)
                turn_perm(pair, next_started=prepare)
                gather(pair, 10)

            keys(Pair(0, 0))
            prepare_all(Pair(0, 0))
            keys(Pair(0, 1))
            body(Pair(0, 0), finish=False)
            body(Pair(0, 1))
            with eng.Fori(1, PAIRS // 2 - 1) as i:
                body(Pair(i, 0))
                body(Pair(i, 1))
            body(Pair(0, PAIRS - 2), order=False)
            body(Pair(0, PAIRS - 1), order=False, prepare=False)
            project(Pair(0, PAIRS - 1))
            unsort_y(Pair(0, PAIRS - 1))

            def general(pair):
                keys(pair)
                prepare_all(pair)
                with eng.Fori(0, N) as s:
                    eng.wait_ge(vl_ready, 2 * (pair.n + 1))
                    eng.wait_ge(general_hot, pair.data * N + s + 1)
                    gather_into(pair.side, ring[0], "main", lambda c: hot[0][:, c, 0:N], N)
                    gather_into(pair.side, ring[1], "tail", lambda c: hot[0][:, c, 0:N], N
                                ).then_inc(general_gathered, 1)
                project(pair)
                turn_perm(pair, next_started=False)
                unsort_y(pair)

            general_loop(eng, general)

        @block.vector
        def _(eng):
            eng.memset(over_sum[:, :], 0.0).then_inc(over_added, 1)
            for half in range(2):
                other = slice((1 - half) * HT, (2 - half) * HT)
                eng.memset(w2t[other, half, :], 0.0).then_inc(weights_ready, 1)
            eng.memset(ones[:, :], 1.0).then_inc(consts_ready, 1)
            eng.memset(ones32[:, :], 1.0).then_inc(weights_ready, 1)
            eng.wait_ge(consts_ready, 7)

            def masks(pair):
                eng.wait_ge(adj_loaded[pair.side], 16 * (pair.half + 1))
                if pair.follows(2):
                    eng.wait_ge(excess_ready, pair.n - 1)
                eng.tensor_scalar(mask[pair.side][:, :, :], adj_sb[pair.side][:, :, :], 0.0, None,
                                  ALU.is_gt).then_inc(masks_ready, 1)

            def degree_keys(pair):
                eng.wait_ge(degrees_ready, TILES * (pair.n + 1))
                eng.tensor_copy(deg16[pair.side][:, :], deg[pair.side][:, :]).then_inc(degrees_copied, 1)
                if pair.follows(1):
                    eng.wait_ge(ranks_ready, pair.n)
                eng.scalar_tensor_tensor(out=neg_key[:, :], in0=deg[pair.side][:, :], scalar=-1.0,
                                         in1=const("neg_tie_col"), op0=ALU.mult,
                                         op1=ALU.add).then_inc(degrees_copied, 1)

            def permutation(pair):
                eng.wait_ge(ranks_ready, pair.n + 1)
                if pair.follows(2):
                    eng.wait_ge(permT_ready, pair.n - 1)
                for c in range(TILES):
                    last = eng.tensor_scalar(perm[pair.side][:, c, :], signs[:, :], rank[:, c:c + 1], None,
                                             ALU.is_equal)
                last.then_inc(perm_ready, 1)

            def scale_weights():
                eng.wait_ge(weights_loaded, 16 * 9)
                eng.scalar_tensor_tensor(out=w_abs[:, :], in0=w1b[:, :], scalar=-1.0, in1=w1b[:, :],
                                         op0=ALU.mult, op1=ALU.max).then_inc(scale_step, 1)
                for c in range(X_CHUNKS):
                    eng.wait_ge(x_all_loaded[c], 16)
                    eng.tensor_reduce(x_max[:, c:c + 1], x_all[:, c, :], AX.X, ALU.max,
                                      apply_absolute_value=True).then_inc(scale_step, 1)
                eng.wait_ge(scale_step, X_CHUNKS + 1)
                eng.tensor_reduce(x_max1[:, :], x_max[:, :], AX.X, ALU.max).then_inc(scale_step, 1)
                eng.wait_ge(w_sums_ready, 1)
                eng.tensor_reduce(w_top[:, :], ring[0][:, 0:H], AX.X, ALU.max).then_inc(scale_step, 1)
                eng.wait_ge(x_turned, 1)
                eng.tensor_reduce(x_top[:, :], ring[1][0:1, 0:P], AX.X, ALU.max).then_inc(scale_step, 1)
                eng.wait_ge(x_top_spread, 1)
                eng.wait_ge(scale_step, X_CHUNKS + 4)
                eng.tensor_tensor(bound[:, :], ring[2][:, 0:1], w_top[:, :], ALU.mult).then_inc(scale_step, 1)
                eng.wait_ge(scale_step, X_CHUNKS + 5)
                eng.tensor_scalar(bound1[:, :], bound[:, :], LEAST_BOUND, None, ALU.max).then_inc(scale_step, 1)
                eng.wait_ge(scale_step, X_CHUNKS + 6)
                eng.tensor_scalar(power[:, :], bound1[:, :].bitcast(I32), EXPONENT, None,
                                  ALU.bitwise_and).then_inc(scale_step, 1)
                eng.wait_ge(scale_step, X_CHUNKS + 7)
                eng.tensor_scalar(up_bits[:, :], power[:, :], -1.0, float((2 * BIAS + TOP - 1) << MANTISSA),
                                  ALU.mult, ALU.add).then_inc(scale_step, 1)
                eng.tensor_scalar(down[:, :], power[:, :].bitcast(F32), 2.0 ** (1 - TOP), None,
                                  ALU.mult).then_inc(scale_step, 1)
                eng.tensor_tensor(w1s[:, :], w1a[:, :], w1b[:, :], ALU.add).then_inc(scale_step, 1)
                eng.wait_ge(scale_step, X_CHUNKS + 10)
                up = up_bits[:, :].bitcast(F32)
                eng.tensor_scalar(w1n[:, :], w1b[:, :], up[0:F, :], -1.0, ALU.mult, ALU.mult
                                  ).then_inc(weights_ready, 1)
                eng.tensor_scalar(w1ab[:, :], w1s[:, :], up[0:F, :], None, ALU.mult).then_inc(weights_ready, 1)
                eng.tensor_scalar(b1ms[:, :], b1m[:, :], up, None, ALU.mult).then_inc(weights_ready, 1)
                eng.tensor_scalar(b1ts[:, :], b1t[:, :], up, None, ALU.mult).then_inc(weights_ready, 1)
                eng.wait_ge(weights_ready, 2)
                eng.tensor_scalar(w2ms[:, :], w2m[:, :], down[:, 0:1], None, ALU.mult).then_inc(weights_ready, 1)
                eng.tensor_scalar(w2ts[:, :, :], w2t[:, :, :], down[:, 0:1], None, ALU.mult).then_inc(weights_ready, 1)

            def start_sums(pair):
                eng.wait_ge(u_copied, 2 * (pair.n + 1))
                eng.wait_ge(excess_ready, pair.n + 1)
                if not pair.general:
                    eng.wait_ge(over_ready, pair.n + 1)
                if pair.follows(2):
                    eng.wait_ge(y_ready, pair.n - 1)
                side = pair.side
                if pair.general:
                    eng.memset(sm[side][:, :, :], 0.0).then_inc(sums_started, 2)
                    eng.memset(st[side][:, :], 0.0).then_inc(sums_started, 1)
                    return
                eng.scalar_tensor_tensor(out=sm[side][:, :, :].rearrange("p g r -> p (g r)"),
                                         in0=um[side][:, :, :].rearrange("p g r -> p (g r)"), scalar=0.0,
                                         in1=bx3[:, :], op0=ALU.max, op1=ALU.mult).then_inc(sums_started, 1)
                for g in range(2):
                    rows = slice(g * HT, g * HT + HT)
                    eng.scalar_tensor_tensor(out=st[side][rows, :], in0=ut[side][rows, :], scalar=0.0,
                                             in1=bx3[rows, g * N:g * N + N], op0=ALU.max,
                                             op1=ALU.mult).then_inc(sums_started, 1)

            def selections(pair, first, last):
                if first == 0:
                    eng.wait_ge(slots_copied, 2 * (pair.n + 1))
                    if pair.follows(2):
                        eng.wait_ge(gathered, NU * (pair.n - 1))
                side = pair.side
                for s in range(first, last):
                    c0, n = START[s], CAPS[s]
                    if s < BIG_SLOTS:
                        eng.tensor_scalar(hot[side][:, :, c0:c0 + n], slotT[:, :, 0:n], float(MARK + s), None,
                                          ALU.is_equal).then_inc(hot_ready, 1)
                    else:
                        eng.tensor_tensor(
                            hot[side][:, :, c0:].rearrange("p c (s r) -> p c s r", r=SMALL),
                            slotT[:, :, 0:SMALL].unsqueeze(2).broadcast_to([P, TILES, NSMALL, SMALL]),
                            small_marks[:, :].rearrange("p (s r) -> p s r", r=SMALL).unsqueeze(1)
                            .broadcast_to([P, TILES, NSMALL, SMALL]),
                            ALU.is_equal).then_inc(hot_ready, 1)

            def views(pair, unit, segment, b, start=0):
                tile, s0, _, _ = UNITS[unit]
                _, n = unit_cols(unit)
                first, slots = segment
                c = START[first] - START[s0]
                cap = CAPS[first]
                if tile == "main":
                    v = b[:, 0:2 * n].rearrange("p (g c) -> p g c", g=2)[:, :, c:c + slots * cap]
                    return v.rearrange("p g (s r) -> p g s r", r=cap)
                return b[:, c:c + slots * cap].rearrange("p (s r) -> p s r", r=cap)

            def shift(pair, unit):
                tile = UNITS[unit][0]
                side = pair.side
                eng.wait_ge(gathered, NU * pair.n + unit + 1)
                b, to = ring[unit % BANKS], tmp[unit % NTMP]
                for first, slots in UNITS[unit][3]:
                    cap = CAPS[first]
                    if tile == "main":
                        u = um[side][:, :, 0:cap].unsqueeze(2).broadcast_to([P, 2, slots, cap])
                    else:
                        u = ut[side][:, 0:cap].unsqueeze(1).broadcast_to([P, slots, cap])
                    eng.tensor_tensor(views(pair, unit, (first, slots), to), views(pair, unit, (first, slots), b),
                                      u, ALU.add).then_inc(shifted, 1)

            def add(pair, unit):
                tile = UNITS[unit][0]
                side = pair.side
                sums = sm[side] if tile == "main" else st[side]
                t = tmp[unit % NTMP]
                eng.wait_ge(shifted, NSHIFT * pair.n + SHIFTS_BEFORE[unit + 1])
                if unit == 0:
                    eng.wait_ge(sums_started, 3 * (pair.n + 1))
                done = ADDS_BEFORE[unit]
                for first, slots in UNITS[unit][3]:
                    if first >= BIG_SLOTS:
                        continue
                    cap = CAPS[first]
                    v = views(pair, unit, (first, slots), t)
                    for s in range(slots):
                        to = sums[:, :, 0:cap] if tile == "main" else sums[:, 0:cap]
                        if done or pair.follows(1):
                            eng.wait_ge(added, NADD * pair.n + done)
                        eng.scalar_tensor_tensor(out=to, in0=v[:, :, s, :] if tile == "main" else v[:, s, :],
                                                 scalar=0.0, in1=to, op0=ALU.max, op1=ALU.add).then_inc(added, 1)
                        done += 1

            def small_views(pair, unit):
                side = pair.side
                v = views(pair, unit, (BIG_SLOTS, NSMALL), tmp[unit % NTMP])
                if UNITS[unit][0] == "main":
                    return v, v.rearrange("p g s r -> p g r s"), small_sum[:, :, :], sm[side][:, :, 0:SMALL], 1
                return v, v.rearrange("p s r -> p r s"), small_sum_t[:, :], st[side][:, 0:SMALL], 0

            def clamp_small(pair, unit):
                v, _, _, _, k = small_views(pair, unit)
                eng.wait_ge(shifted, NSHIFT * pair.n + SHIFTS_BEFORE[unit + 1])
                eng.tensor_scalar(v, v, 0.0, None, ALU.max).then_inc(clamped, 1)

            def reduce_small(pair, unit):
                _, turned, part, _, k = small_views(pair, unit)
                eng.wait_ge(clamped, 2 * pair.n + k + 1)
                eng.tensor_reduce(part, turned, AX.X, ALU.add).then_inc(reduced, 1)

            def add_small(pair, unit):
                _, _, part, to, k = small_views(pair, unit)
                eng.wait_ge(reduced, 2 * pair.n + k + 1)
                eng.wait_ge(added, NADD * pair.n + ADDS_BEFORE[unit + 1] - 1)
                eng.tensor_tensor(to, to, part, ALU.add).then_inc(added, 1)

            def normalise(pair):
                side = pair.side
                eng.wait_ge(z_ready, pair.n + 1)
                eng.wait_ge(xb_ready, pair.n + 1)
                if pair.follows(1):
                    eng.wait_ge(centred_ready, pair.n)
                zf = z[:, :, :].rearrange("p t o -> p (t o)")
                eng.tensor_tensor(zf, by[:, TILES * O:2 * TILES * O],
                                  xb[side][:, :, :].rearrange("p t f -> p (t f)"), ALU.add).then_inc(z_added, 1)
                eng.wait_ge(z_added, pair.n + 1)
                for c in range(TILES):
                    eng.bn_stats(stats[:, c, :], z[:, c, :]).then_inc(stats_ready, 1)
                eng.wait_ge(stats_ready, TILES * (pair.n + 1))
                eng.tensor_tensor(apart[:, :], stats[:, :, 1], stats[:, :, 4], ALU.subtract).then_inc(moments_ready, 1)
                eng.tensor_tensor(within[:, :], stats[:, :, 2], stats[:, :, 5], ALU.add).then_inc(moments_ready, 1)
                eng.wait_ge(moments_ready, 4 * pair.n + 1)
                eng.scalar_tensor_tensor(out=mean[:, :], in0=apart[:, :], scalar=-0.5, in1=stats[:, :, 1],
                                         op0=ALU.mult, op1=ALU.add).then_inc(mean_ready, 1)
                eng.scalar_tensor_tensor(out=across[:, :], in0=apart[:, :], scalar=O / 4.0, in1=apart[:, :],
                                         op0=ALU.mult, op1=ALU.mult).then_inc(moments_ready, 1)
                eng.wait_ge(moments_ready, 4 * pair.n + 3)
                eng.tensor_tensor(spread[:, :], within[:, :], across[:, :], ALU.add).then_inc(moments_ready, 1)

            def inverse_deviation(pair):
                eng.wait_ge(std_ready, pair.n + 1)
                if pair.follows(1):
                    eng.wait_ge(normed, pair.n)
                eng.reciprocal(rstd[:, :], std[:, :]).then_inc(rstd_ready, 1)

            def order_nodes(pair):
                masks(pair)
                degree_keys(pair)

            def prepare_all(pair):
                permutation(pair)
                if not pair.follows(1):
                    scale_weights()
                start_sums(pair)
                if not pair.general:
                    selections(pair, 0, NHOT)

            def body(pair, order=True, prepare=True, finish=True):
                new, old, second = pair.at(1), pair.at(-1), pair.at(2)
                if prepare:
                    permutation(new)
                shift(pair, 0)
                shift(pair, 1)
                add(pair, 0)
                if order:
                    masks(second)
                shift(pair, 2)
                add(pair, 1)
                shift(pair, 3)
                add(pair, 2)
                if prepare:
                    selections(new, 0, 1)
                shift(pair, 4)
                add(pair, 3)
                if prepare:
                    selections(new, 1, 3)
                shift(pair, 5)
                if order:
                    degree_keys(second)
                add(pair, 4)
                if finish:
                    normalise(old)
                shift(pair, 6)
                add(pair, 5)
                if prepare:
                    selections(new, 3, 5)
                if finish:
                    inverse_deviation(old)
                shift(pair, 7)
                add(pair, 6)
                if prepare:
                    start_sums(new)
                shift(pair, 8)
                add(pair, 7)
                if prepare:
                    selections(new, 5, 6)
                clamp_small(pair, 8)
                add(pair, 8)
                shift(pair, 9)
                reduce_small(pair, 8)
                if prepare:
                    selections(new, 6, 8)
                add_small(pair, 8)
                shift(pair, 10)
                add(pair, 9)
                clamp_small(pair, 10)
                add(pair, 10)
                if prepare:
                    selections(new, 8, 9)
                reduce_small(pair, 10)
                if prepare:
                    selections(new, 9, NHOT)
                add_small(pair, 10)

            order_nodes(Pair(0, 0))
            masks(Pair(0, 1))
            prepare_all(Pair(0, 0))
            degree_keys(Pair(0, 1))
            body(Pair(0, 0), finish=False)
            body(Pair(0, 1))
            with eng.Fori(1, PAIRS // 2 - 1) as i:
                body(Pair(i, 0))
                body(Pair(i, 1))
            body(Pair(0, PAIRS - 2), order=False)
            body(Pair(0, PAIRS - 1), order=False, prepare=False)
            normalise(Pair(0, PAIRS - 1))
            inverse_deviation(Pair(0, PAIRS - 1))

            def general(pair):
                side = pair.side
                order_nodes(pair)
                prepare_all(pair)
                sf = sm[side][:, :, :].rearrange("p g r -> p (g r)")
                uf = um[side][:, :, :].rearrange("p g r -> p (g r)")
                tail = tmp[1][:, 0:N]
                with eng.Fori(0, N) as s:
                    number = pair.data * N + s
                    done = number * GENERAL_STEPS
                    mark = const("marks")[:, bass.ds(s, 1)]
                    slot = const("iota")[:, bass.ds(s, 1)]
                    eng.wait_ge(slots_copied, 2 * (pair.n + 1))
                    eng.wait_ge(sums_started, 3 * (pair.n + 1))
                    eng.tensor_scalar(hot[0][:, :, 0:N], slotT[:, :, :], mark, None,
                                      ALU.is_equal).then_inc(general_hot, 1)
                    eng.wait_ge(general_gathered, number + 1)
                    eng.tensor_tensor(tmp[0][:, :], ring[0][:, :], uf, ALU.add).then_inc(general_step, 1)
                    eng.tensor_tensor(tail, ring[1][:, 0:N], ut[side][:, :], ALU.add).then_inc(general_step, 1)
                    eng.wait_ge(general_step, done + 2)
                    eng.scalar_tensor_tensor(out=tmp[0][:, :], in0=bx3[:, :], scalar=slot, in1=tmp[0][:, :],
                                             op0=ALU.is_gt, op1=ALU.mult).then_inc(general_step, 1)
                    for g in range(2):
                        rows = slice(g * HT, g * HT + HT)
                        eng.scalar_tensor_tensor(out=tail[rows, :], in0=bx3[rows, g * N:g * N + N],
                                                 scalar=slot[rows, :], in1=tail[rows, :],
                                                 op0=ALU.is_gt, op1=ALU.mult).then_inc(general_step, 1)
                    eng.wait_ge(general_step, done + 5)
                    eng.scalar_tensor_tensor(out=sf, in0=tmp[0][:, :], scalar=0.0, in1=sf,
                                             op0=ALU.max, op1=ALU.add).then_inc(general_step, 1)
                    eng.scalar_tensor_tensor(out=st[side][:, :], in0=tail, scalar=0.0, in1=st[side][:, :],
                                             op0=ALU.max, op1=ALU.add).then_inc(general_step, 1)
                    eng.wait_ge(general_step, done + GENERAL_STEPS)
                    eng.tensor_copy(idle[:, :], std[:, 0:1])
                normalise(pair)
                inverse_deviation(pair)

            general_loop(eng, general)


def kernel(**inputs):
    import concourse.bacc as bacc
    from concourse.bass_utils import run_bass_kernel_spmd

    nc = bacc.Bacc("TRN2", target_bir_lowering=False, num_devices=1)
    x = np.ascontiguousarray(inputs["x"])
    arrays = {
        "x": x,
        "xT": np.ascontiguousarray(x.reshape(GRAPHS * N, F).T),
        "adj": np.ascontiguousarray(inputs["adj"]),
        "w1": np.ascontiguousarray(inputs["L0_gnn_W1"]),
        "b1": np.ascontiguousarray(inputs["L0_gnn_b1"]),
        "w2": np.ascontiguousarray(inputs["L0_gnn_W2"]),
        "b2": np.ascontiguousarray(inputs["L0_gnn_b2"]),
        "consts": constants(),
    }
    args = [nc.dram_tensor(name, a.shape, mybir.dt.from_np(a.dtype), kind="ExternalInput").ap()
            for name, a in arrays.items()]
    out = nc.dram_tensor("out", (GRAPHS, N, F), F32, kind="ExternalOutput").ap()
    build(nc, *args, out)
    return run_bass_kernel_spmd(nc, [arrays], core_ids=[0]).results[0]["out"]
```

```python
from contextlib import ExitStack

import numpy as np

import concourse.bass as bass
from concourse import mybir

ALU = mybir.AluOpType
ACT = mybir.ActivationFunctionType
F32 = mybir.dt.float32
BF16 = mybir.dt.bfloat16
F16 = mybir.dt.float16
I32 = mybir.dt.int32
AX = mybir.AxisListType

GRAPHS, N, F, H, O = 32, 256, 64, 192, 64
EPS = 1e-5
P = 128
NT = N // P
PAIRS = GRAPHS // 2
HT = H - P
TILES = 2 * NT
X_CHUNKS = 4
TOP = 13
LEAST_BOUND = 2.0 ** -80
EXPONENT = 0x7F800000
BIAS, MANTISSA = 127, 23
MARK = 2 * N

SMALL, NSMALL = 16, 8
CAPS = [256, 256, 256, 224, 176, 120, 80, 48, 48] + [SMALL] * NSMALL
START = [sum(CAPS[:s]) for s in range(len(CAPS))]
COLS = sum(CAPS)
BIG_SLOTS = len(CAPS) - NSMALL


def slots_given(rank):
    return sum(c > rank for c in CAPS)


UNITS = [
    ("main", 0, 1, [(0, 1)]),
    ("tail", 0, 2, [(0, 2)]),
    ("main", 1, 2, [(1, 1)]),
    ("tail", 2, 4, [(2, 1), (3, 1)]),
    ("main", 2, 3, [(2, 1)]),
    ("tail", 4, 7, [(4, 1), (5, 1), (6, 1)]),
    ("main", 3, 4, [(3, 1)]),
    ("main", 4, 5, [(4, 1)]),
    ("tail", 7, 17, [(7, 2), (9, 8)]),
    ("main", 5, 7, [(5, 1), (6, 1)]),
    ("main", 7, 17, [(7, 2), (9, 8)]),
]
NU = len(UNITS)
BANKS = 3


def unit_cols(unit):
    _, s0, s1, _ = UNITS[unit]
    return START[s0], sum(CAPS[s0:s1])


def adds_of(unit):
    return sum(1 if s0 >= BIG_SLOTS else n for s0, n in UNITS[unit][3])


ON_VECTOR = 2

SHIFTS = [len(u[3]) for u in UNITS]
SHIFTS_BEFORE = [sum(SHIFTS[:u]) for u in range(NU + 1)]
NSHIFT = SHIFTS_BEFORE[NU]
ADDS_BEFORE = [sum(adds_of(i) for i in range(u) if UNITS[i][0] == UNITS[u][0]) for u in range(NU)]
ADDS = {tile: sum(adds_of(i) for i in range(NU) if UNITS[i][0] == tile) for tile in ("main", "tail")}
NHOT = BIG_SLOTS + 1

GENERAL_STEPS = 7

CONSTS = {}


def constants():
    p = np.arange(P)[:, None]
    node = np.arange(TILES * P)[None, :] % N
    arrays = dict(
        half=(np.float16, dict(
            signs=np.broadcast_to(2 * np.arange(N)[None, :] - (N - 1), (P, N)),
            ident16=np.eye(P),
            before=(p < np.arange(P)[None, :]) + MARK * np.eye(P),
            small_marks=np.broadcast_to(
                np.repeat(MARK + BIG_SLOTS + np.arange(NSMALL), SMALL)[None, :], (P, NSMALL * SMALL)))),
        row=(np.float16, dict(
            tie_row=(N - 1 - node) / N,
            neg_given=np.array([[-slots_given(r) for r in range(N)] * 2]))),
        single=(np.float32, dict(
            per_output=np.full((P, TILES), 1.0 / O),
            neg_tie_col=-(N - 1 - (np.arange(TILES)[None, :] % NT * P + p)) / N,
            eps=np.full((P, 1), EPS),
            ident32=np.eye(P))),
        general=(np.float32, dict(
            marks=np.broadcast_to(MARK + np.arange(N)[None, :], (P, N)),
            iota=np.broadcast_to(np.arange(N)[None, :], (P, N)))),
    )
    out = {}
    for array, (dtype, parts) in arrays.items():
        at = 0
        for name, a in parts.items():
            CONSTS[name] = (array, at, a.shape[1])
            at += a.shape[1]
        out[array] = np.ascontiguousarray(np.concatenate(list(parts.values()), axis=1).astype(dtype))
    return out


WEIGHTS = dict(w1a=(0, 2 * H), w1b=(2 * H, 2 * H), b1m=(4 * H, 1), b1t=(4 * H + 1, 1), w2m=(4 * H + 2, O),
               w2t=(4 * H + 2 + O, 2 * O), b2b=(4 * H + 2 + 3 * O, O))
WEIGHT_COLS = 4 * H + 2 + 4 * O


def lay_out_weights(w1, b1, w2, b2):
    def per_graph(a):
        both = np.zeros((2, P // 2, 2, a.shape[1]), np.float32)
        for g in range(2):
            both[g, :, g] = a
        return both.reshape(P, -1)

    def hidden(a):
        return np.concatenate([per_graph(a[:, :P]), per_graph(a[:, P:])], axis=1)

    parts = dict(
        w1a=hidden(w1[:F]), w1b=hidden(w1[F:]), b1m=b1[:P, None], b1t=np.tile(b1[P:, None], (2, 1)),
        w2m=w2[:P], w2t=per_graph(w2[P:]), b2b=np.broadcast_to(b2[None, :], (P, O)))
    return np.ascontiguousarray(np.concatenate([parts[name] for name in WEIGHTS], axis=1))


class Pair:

    def __init__(self, i, offset, general=False):
        base = PAIRS if general else 0
        self.n = 2 * i + (offset + base)
        self.half = i + (offset + base) // 2
        self.side = offset % 2
        self.data = 2 * i + offset
        self.general = general
        self.i, self.offset = i, offset

    def follows(self, k):
        return not isinstance(self.n, int) or self.n >= k

    def at(self, distance):
        return Pair(self.i, self.offset + distance, self.general)


def build(nc, x, xT, adj, weights, half, row, single, general_consts, out):
    x_v = x.rearrange("(g two) (t p) f -> g p (two t) f", two=2, p=P)
    adj_v = adj.rearrange("(g two) (t p) k -> g p (two t) k", two=2, p=P)
    out_v = out.rearrange("(g two) (t p) f -> g p (two t) f", two=2, p=P)

    with ExitStack() as ctx:
        def sb(name, shape, dt=F32):
            return ctx.enter_context(nc.sbuf_tensor(name, shape, dt))

        def bank(name):
            return ctx.enter_context(nc.psum_tensor(name, [P, 512], F32))

        def sem(name):
            return ctx.enter_context(nc.semaphore(name))

        def both(name, shape, dt=F32):
            return [sb(f"{name}{s}", shape, dt) for s in range(2)]

        cst = {name: sb(f"cst_{name}", a.shape, a.dtype)
               for name, a in (("half", half), ("row", row), ("single", single), ("general", general_consts))}

        def const(name):
            array, at, n = CONSTS[name]
            return cst[array][:, at:at + n]

        signs = const("signs")
        tie_row, neg_given = const("tie_row"), const("neg_given")
        before, small_marks = const("before"), const("small_marks")
        ident = sb("ident", [P, P], BF16)
        ones = sb("ones", [P, P], BF16)
        wts = sb("wts", [P, WEIGHT_COLS])

        def weight(name):
            at, n = WEIGHTS[name]
            return wts[:, at:at + n]

        w1a, w1b = weight("w1a"), weight("w1b")
        b1m, b1t = weight("b1m"), weight("b1t")
        w2m = weight("w2m")
        w2t = weight("w2t").rearrange("p (g o) -> p g o", g=2)
        b2b = weight("b2b")
        w1ab = sb("w1ab", [P, 2 * H])
        w1n = sb("w1n", [P, H])
        ones32 = sb("ones32", [P, P])
        x_all = sb("x_all", [P, X_CHUNKS, GRAPHS * N * F // P // X_CHUNKS])
        x_max = sb("x_max", [P, X_CHUNKS])
        x_max1 = sb("x_max1", [P, 1])
        x_top = sb("x_top", [1, 1])
        w_abs = sb("w_abs", [P, 2 * H])
        w_top = sb("w_top", [P, 1])
        bound = sb("bound", [P, 1])
        bound1 = sb("bound1", [P, 1])
        power = sb("power", [P, 1], I32)
        up_bits = sb("up_bits", [P, 1], I32)
        down = sb("down", [P, 1])
        w1s = sb("w1s", [P, 2 * H])
        b1ms, b1ts = sb("b1ms", [P, 1]), sb("b1ts", [P, 1])
        w2ms, w2ts = sb("w2ms", [P, O]), sb("w2ts", [P, 2, O])
        adj_sb = both("adj_sb", [P, TILES, N])
        x_sb = both("x_sb", [P, TILES, F])
        xT_sb = both("xT_sb", [P, N])
        mask = both("mask", [P, TILES, N], BF16)
        deg = both("deg", [P, TILES])
        deg16 = both("deg16", [P, TILES], BF16)
        neg_key = sb("neg_key", [P, TILES])
        rank = sb("rank", [P, TILES])
        adj_sign = sb("adj_sign", [P, TILES, N], BF16)
        junk2 = sb("junk2", [P, TILES, N], BF16)
        distance = sb("distance", [P, TILES, N], BF16)
        perm = both("perm", [P, TILES, N], BF16)
        permT = both("permT", [P, TILES, N])
        maskT = sb("maskT", [P, TILES, N], BF16)
        slotT = sb("slotT", [P, TILES, N], F16)
        hot = both("hot", [P, TILES, COLS], BF16)
        excess_junk = sb("excess_junk", [1, 2 * N])
        over = sb("over", [1, 1])
        over_sum = sb("over_sum", [1, 1])
        over_int = sb("over_int", [1, 1], I32)
        xb = both("xb", [P, TILES, F])
        db = both("db", [P, TILES, F])
        xh = sb("xh", [P, TILES, F], BF16)
        xm = sb("xm", [P, TILES, F], BF16)
        xl = sb("xl", [P, TILES, F], BF16)
        xr = sb("xr", [P, TILES, F])
        xs = sb("xs", [P, N])
        vh = both("vh", [P, TILES, H], F16)
        vl = both("vl", [P, TILES, H], F16)
        um = both("um", [P, 2, N])
        ut = both("ut", [P, N])
        sm = both("sm", [P, 2, N])
        st = both("st", [P, N])
        NTMP = 3
        tmp = [sb(f"tmp{i}", [P, 512]) for i in range(NTMP)]
        small_sum, small_sum_t = sb("small_sum", [P, 2, SMALL]), sb("small_sum_t", [P, SMALL])
        vf = sb("vf", [P, TILES, H])
        y_sb = sb("y_sb", [P, TILES, O])
        z = sb("z", [P, TILES, O])
        z_sum = sb("z_sum", [P, TILES])
        mean = sb("mean", [P, TILES])
        spread = sb("spread", [P, TILES])
        std = sb("std", [P, TILES])
        rstd = sb("rstd", [P, TILES])
        centred = sb("centred", [P, TILES, O])
        z_junk = sb("z_junk", [P, TILES, O])
        idle, idle_act = sb("idle", [P, 1]), sb("idle_act", [P, 1])
        o_sb = both("o_sb", [P, TILES, O])

        bx0, bx1, bx2, bx3 = (bank(f"bx{i}") for i in range(4))
        by = bank("by")
        ring = [bank(f"ring{i}") for i in range(BANKS)]

        consts_loaded = {name: sem(f"{name}_loaded") for name in cst}
        weights_loaded = sem("weights_loaded")
        consts_ready, weights_ready = sem("consts_ready"), sem("weights_ready")
        x_all_loaded = [sem(f"x_all_loaded{c}") for c in range(X_CHUNKS)]
        w1s_ready = sem("w1s_ready")
        scale_step = sem("scale_step")
        w_sums_ready, x_turned, x_top_spread = sem("w_sums_ready"), sem("x_turned"), sem("x_top_spread")
        adj_loaded = [sem(f"adj_loaded{s}") for s in range(2)]
        x_loaded = [sem(f"x_loaded{s}") for s in range(2)]
        xT_loaded = [sem(f"xT_loaded{s}") for s in range(2)]
        stored = [sem(f"stored{s}") for s in range(2)]
        signs_ready = sem("signs_ready")
        degrees_ready = sem("degrees_ready")
        deg16_ready, neg_keys_ready = sem("deg16_ready"), sem("neg_keys_ready")
        keys_ready = sem("keys_ready")
        ranks_ready = sem("ranks_ready")
        distances_ready, perm_ready = sem("distances_ready"), sem("perm_ready")
        maskT_ready = sem("maskT_ready")
        maskT_copied = sem("maskT_copied")
        slots_ready = sem("slots_ready")
        slots_copied = sem("slots_copied")
        excess_ready = sem("excess_ready")
        over_ready = sem("over_ready")
        over_added = sem("over_added")
        db_ready, xb_ready = sem("db_ready"), sem("xb_ready")
        xh_ready, xr_ready = sem("xh_ready"), sem("xr_ready")
        xm_ready, xl_ready = sem("xm_ready"), sem("xl_ready")
        xs_ready, xs_copied = sem("xs_ready"), sem("xs_copied")
        u_ready, u_copied = sem("u_ready"), sem("u_copied")
        v_ready, vh_ready = sem("v_ready"), sem("vh_ready")
        vf_ready, vl_ready = sem("vf_ready"), sem("vl_ready")
        sums_started = sem("sums_started")
        hot_ready = sem("hot_ready")
        gathered = sem("gathered")
        shifted = sem("shifted")
        clamped, reduced = sem("clamped"), sem("reduced")
        added = {"main": sem("added_main"), "tail": sem("added_tail")}
        permT_ready, permT_copied = sem("permT_ready"), sem("permT_copied")
        y_ready, y_copied = sem("y_ready"), sem("y_copied")
        z_ready, z_added = sem("z_ready"), sem("z_added")
        z_summed, squares_ready = sem("z_summed"), sem("squares_ready")
        std_ready, rstd_ready = sem("std_ready"), sem("rstd_ready")
        mean_ready, centred_ready = sem("mean_ready"), sem("centred_ready")
        normed = sem("normed")
        over_all = sem("over_all")
        general_hot, general_gathered = sem("general_hot"), sem("general_gathered")
        general_step = sem("general_step")

        block = ctx.enter_context(nc.Block())

        def general_loop(eng, body, after=None):
            eng.wait_ge(over_all, 1)
            needed = eng.value_load(over_int[0:1, 0:1], min_val=0, max_val=GRAPHS * N * N)
            with eng.If(needed > 0):
                with eng.Fori(0, PAIRS // 2) as i:
                    for side in range(2):
                        pair = Pair(i, side, general=True)
                        eng.wait_ge(normed, pair.n)
                        body(pair)
                if after:
                    after()

        @block.sync
        def _(eng):
            def load_adj(pair):
                if not pair.general and pair.follows(2):
                    eng.wait_ge(signs_ready, pair.n - 1)
                eng.dma_start(adj_sb[pair.side][:, :, :], adj_v[pair.data]).then_inc(adj_loaded[pair.side], 16)

            def load_xT(pair):
                if not pair.general and pair.follows(2):
                    eng.wait_ge(v_ready, 2 * (pair.n - 1))
                eng.dma_start(xT_sb[pair.side][:, :], xT[pair.data]).then_inc(xT_loaded[pair.side], 16)

            def load_x(pair):
                if not pair.general and pair.follows(2):
                    eng.wait_ge(xb_ready, pair.n - 1)
                eng.dma_start(x_sb[pair.side][:, :, :], x_v[pair.data]).then_inc(x_loaded[pair.side], 16)

            def store(pair):
                eng.wait_ge(normed, pair.n + 1)
                eng.dma_start(out_v[pair.data], o_sb[pair.side][:, :, :]).then_inc(stored[pair.side], 16)

            def body(pair, first=False):
                load_adj(pair)
                load_xT(pair.at(-1))
                load_x(pair)
                if not first:
                    store(pair.at(-5))

            load_adj(Pair(0, 0))
            eng.dma_start(cst["half"][:, :], half[:, :]).then_inc(consts_loaded["half"], 16)
            eng.dma_start(cst["row"][:, :], row[:, :]).then_inc(consts_loaded["row"], 16)
            eng.dma_start(cst["single"][:, :], single[:, :]).then_inc(consts_loaded["single"], 16)
            load_x(Pair(0, 0))
            eng.dma_start(wts[:, :], weights[:, :]).then_inc(weights_loaded, 16)
            x_all_v = x.rearrange("g n f -> (g n f)").rearrange("(p c m) -> p c m", p=P, c=X_CHUNKS)
            for c in range(X_CHUNKS):
                eng.dma_start(x_all[:, c, :], x_all_v[:, c, :]).then_inc(x_all_loaded[c], 16)
            load_adj(Pair(0, 1))
            load_x(Pair(0, 1))
            load_xT(Pair(0, 0))
            eng.dma_start(cst["general"][:, :], general_consts[:, :]).then_inc(consts_loaded["general"], 16)
            load_adj(Pair(0, 2))
            load_xT(Pair(0, 1))
            load_x(Pair(0, 2))
            body(Pair(0, 3), first=True)
            body(Pair(0, 4), first=True)
            with eng.Fori(2, PAIRS // 2 - 1) as i:
                body(Pair(i, 1))
                body(Pair(i, 2))
            body(Pair(0, PAIRS - 1))
            load_xT(Pair(0, PAIRS - 1))
            for left in range(5, 0, -1):
                store(Pair(0, PAIRS - left))
            for side in range(2):
                eng.wait_ge(stored[side], 16 * (PAIRS // 2))

            def general(pair):
                load_adj(pair)
                load_xT(pair)
                load_x(pair)
                store(pair)

            def all_stored():
                for side in range(2):
                    eng.wait_ge(stored[side], 16 * PAIRS)

            general_loop(eng, general, all_stored)

        @block.gpsimd
        def _(eng):
            def rest_x(pair):
                eng.wait_ge(xh_ready, pair.n + 1)
                if pair.follows(1):
                    eng.wait_ge(xm_ready, pair.n)
                eng.tensor_tensor(xr[:, :, :], x_sb[pair.side][:, :, :], xh[:, :, :],
                                  ALU.subtract).then_inc(xr_ready, 1)

            def low_x(pair):
                eng.wait_ge(xm_ready, pair.n + 1)
                eng.wait_ge(xr_ready, pair.n + 1)
                eng.tensor_tensor(xl[:, :, :], xr[:, :, :], xm[:, :, :], ALU.subtract).then_inc(xl_ready, 1)

            def degree_bias(pair):
                eng.wait_ge(degrees_ready, TILES * (pair.n + 1))
                if pair.follows(2):
                    eng.wait_ge(xb_ready, pair.n - 1)
                eng.tensor_tensor(db[pair.side][:, :, :], deg[pair.side][:, :].unsqueeze(2).broadcast_to([P, TILES, F]),
                                  b2b.unsqueeze(1).broadcast_to([P, TILES, F]), ALU.mult).then_inc(db_ready, 1)

            def residual(pair):
                eng.wait_ge(db_ready, pair.n + 1)
                if pair.follows(2):
                    eng.wait_ge(z_added, pair.n - 1)
                eng.tensor_tensor(xb[pair.side][:, :, :], db[pair.side][:, :, :], x_sb[pair.side][:, :, :],
                                  ALU.add).then_inc(xb_ready, 1)

            def low_v(pair, g):
                eng.wait_ge(vf_ready, 2 * pair.n + g + 1)
                if not pair.general and pair.follows(2):
                    eng.wait_ge(gathered, NU * (pair.n - 1))
                c = slice(g * NT, g * NT + NT)
                eng.tensor_tensor(vl[pair.side][:, c, :], vf[:, c, :], vh[pair.side][:, c, :],
                                  ALU.subtract).then_inc(vl_ready, 1)

            def count_over(pair):
                eng.wait_ge(over_ready, pair.n + 1)
                eng.wait_ge(over_added, pair.n + 1)
                eng.tensor_tensor(over_sum[:, :], over_sum[:, :], over[:, :], ALU.add).then_inc(over_added, 1)

            def neg_keys(pair):
                eng.wait_ge(degrees_ready, TILES * (pair.n + 1))
                if pair.follows(1):
                    eng.wait_ge(ranks_ready, pair.n)
                eng.tensor_tensor(neg_key[:, :], const("neg_tie_col"), deg[pair.side][:, :],
                                  ALU.subtract).then_inc(neg_keys_ready, 1)

            def centre(pair):
                eng.wait_ge(z_summed, TILES * (pair.n + 1))
                if pair.follows(1):
                    eng.wait_ge(normed, pair.n)
                eng.tensor_tensor(mean[:, :], z_sum[:, :], const("per_output"), ALU.mult).then_inc(mean_ready, 1)
                eng.wait_ge(mean_ready, pair.n + 1)
                eng.tensor_tensor(centred[:, :, :], z[:, :, :],
                                  mean[:, :].unsqueeze(2).broadcast_to([P, TILES, O]), ALU.subtract
                                  ).then_inc(centred_ready, 1)

            def scale(pair):
                eng.wait_ge(rstd_ready, pair.n + 1)
                eng.wait_ge(centred_ready, pair.n + 1)
                if pair.follows(2):
                    eng.wait_ge(stored[pair.side], 16 * pair.half)
                eng.tensor_tensor(o_sb[pair.side][:, :, :], centred[:, :, :],
                                  rstd[:, :].unsqueeze(2).broadcast_to([P, TILES, O]), ALU.mult).then_inc(normed, 1)

            def body(pair, order=True, prepare=True, settle=True):
                if settle:
                    centre(pair.at(-2))
                if order:
                    neg_keys(pair.at(2))
                    degree_bias(pair.at(2))
                    rest_x(pair.at(2))
                if prepare and not pair.general:
                    count_over(pair.at(1))
                if prepare:
                    low_v(pair.at(1), 0)
                    low_v(pair.at(1), 1)
                if settle:
                    scale(pair.at(-2))
                if prepare:
                    residual(pair.at(1))
                if order:
                    low_x(pair.at(2))

            first, next_one = Pair(0, 0), Pair(0, 1)
            eng.wait_ge(consts_loaded["single"], 16)
            neg_keys(first)
            eng.wait_ge(weights_loaded, 16)
            degree_bias(first)
            rest_x(first)
            low_x(first)
            neg_keys(next_one)
            degree_bias(next_one)
            count_over(first)
            low_v(first, 0)
            rest_x(next_one)
            residual(first)
            low_x(next_one)
            body(first, settle=False)
            body(next_one, settle=False)
            with eng.Fori(1, PAIRS // 2 - 1) as i:
                body(Pair(i, 0))
                body(Pair(i, 1))
            body(Pair(0, PAIRS - 2), order=False)
            body(Pair(0, PAIRS - 1), order=False, prepare=False)
            body(Pair(0, PAIRS), order=False, prepare=False)
            body(Pair(0, PAIRS + 1), order=False, prepare=False)
            eng.wait_ge(over_added, PAIRS + 1)
            eng.tensor_copy(over_int[:, :], over_sum[:, :]).then_inc(over_all, 1)

            def general(pair):
                body(pair.at(-2), prepare=False, settle=False)
                body(pair.at(-1), order=False, settle=False)
                body(pair.at(2), order=False, prepare=False)

            general_loop(eng, general)

        @block.scalar
        def _(eng):
            eng.wait_ge(weights_ready, 1)
            eng.activation(idle_act[:, :], ones32[:, 0:1], ACT.Sqrt)

            def adj_signs(pair):
                eng.wait_ge(adj_loaded[pair.side], 16 * (pair.half + 1))
                if pair.follows(1):
                    eng.wait_ge(degrees_ready, TILES * pair.n)
                eng.activation(adj_sign[:, :, :], adj_sb[pair.side][:, :, :], ACT.Sign).then_inc(signs_ready, 1)

            def degrees(pair, g):
                eng.wait_ge(signs_ready, pair.n + 1)
                if pair.follows(2):
                    eng.wait_ge(excess_ready, pair.n - 1)
                    eng.wait_ge(db_ready, pair.n - 1)
                for c in range(g * NT, g * NT + NT):
                    eng.activation(mask[pair.side][:, c, :], adj_sign[:, c, :], ACT.Relu,
                                   accum_out=deg[pair.side][:, c:c + 1]).then_inc(degrees_ready, 1)

            def copy_degrees(pair):
                eng.wait_ge(degrees_ready, TILES * (pair.n + 1))
                if pair.follows(2):
                    eng.wait_ge(excess_ready, pair.n - 1)
                eng.copy(deg16[pair.side][:, :], deg[pair.side][:, :]).then_inc(deg16_ready, 1)

            def ranks(pair):
                eng.wait_ge(keys_ready, pair.n + 1)
                eng.wait_ge(neg_keys_ready, pair.n + 1)
                if pair.follows(1):
                    eng.wait_ge(perm_ready, pair.n)
                for c in range(TILES):
                    g = c // NT
                    last = eng.activation(junk2[:, c, :], bx0[:, g * N:g * N + N], ACT.Sign,
                                          bias=neg_key[:, c:c + 1], accum_out=rank[:, c:c + 1])
                last.then_inc(ranks_ready, 1)

            def permutation(pair):
                eng.wait_ge(ranks_ready, pair.n + 1)
                for c in range(TILES):
                    eng.activation(distance[:, c, :], signs, ACT.Square, scale=-1.0,
                                   bias=rank[:, c:c + 1]).then_inc(distances_ready, 1)
                eng.wait_ge(distances_ready, TILES * (pair.n + 1 - ON_VECTOR))
                if pair.follows(2):
                    eng.wait_ge(permT_ready, pair.n - 1)
                eng.activation(perm[pair.side][:, :, :], distance[:, :, :], ACT.Relu, scale=-1.0,
                               bias=ones32[:, 0:1]).then_inc(perm_ready, 1)

            def high_x(pair):
                eng.wait_ge(x_loaded[pair.side], 16 * (pair.half + 1))
                if pair.follows(1):
                    eng.wait_ge(xs_ready, pair.n)
                eng.copy(xh[:, :, :], x_sb[pair.side][:, :, :]).then_inc(xh_ready, 1)

            def middle_x(pair):
                eng.wait_ge(xr_ready, pair.n + 1)
                eng.copy(xm[:, :, :], xr[:, :, :]).then_inc(xm_ready, 1)

            def copy_maskT(pair):
                for g, b in enumerate((bx1, bx2)):
                    eng.wait_ge(maskT_ready, 2 * pair.n + g + 1)
                    if pair.follows(1):
                        eng.wait_ge(slots_ready, 2 * (pair.n - 1) + g + 1)
                    eng.copy(maskT[:, g * NT:g * NT + NT, :].rearrange("p t r -> p (t r)"),
                             b[:, :]).then_inc(maskT_copied, 1)

            def copy_slots(pair):
                if not pair.general and pair.follows(1):
                    eng.wait_ge(hot_ready, NHOT * pair.n)
                for g, b in enumerate((bx0, bx1)):
                    eng.wait_ge(slots_ready, 2 * pair.n + g + 1)
                    eng.copy(slotT[:, g * NT:g * NT + NT, :].rearrange("p t r -> p (t r)"),
                             b[:, :]).then_inc(slots_copied, 1)

            def look_over(pair):
                eng.wait_ge(excess_ready, pair.n + 1)
                eng.wait_ge(over_added, pair.n + 1)
                eng.activation(excess_junk[:, :], bx3[0:1, :], ACT.Relu, accum_out=over[:, :]).then_inc(over_ready, 1)

            def copy_xs(pair):
                eng.wait_ge(xs_ready, pair.n + 1)
                if pair.follows(1):
                    eng.wait_ge(u_ready, 2 * pair.n)
                eng.copy(xs[:, :], bx2[:, 0:N]).then_inc(xs_copied, 1)

            def copy_u(pair):
                if not pair.general and pair.follows(2):
                    eng.wait_ge(shifted, NSHIFT * (pair.n - 1))
                eng.wait_ge(u_ready, 2 * pair.n + 1)
                eng.activation(um[pair.side][:, :, :].rearrange("p g r -> p (g r)"), bx0[:, :], ACT.Identity,
                               bias=b1ms[:, 0:1]).then_inc(u_copied, 1)
                eng.wait_ge(u_ready, 2 * pair.n + 2)
                eng.activation(ut[pair.side][:, :], bx1[:, 0:N], ACT.Identity,
                               bias=b1ts[:, 0:1]).then_inc(u_copied, 1)

            def high_v(pair, g):
                eng.wait_ge(v_ready, 2 * pair.n + g + 1)
                if not pair.general and pair.follows(2):
                    eng.wait_ge(gathered, NU * (pair.n - 1))
                b = (bx1, bx2)[g]
                eng.copy(vh[pair.side][:, g * NT:g * NT + NT, :].rearrange("p t h -> p (t h)"),
                         b[:, 0:NT * H]).then_inc(vh_ready, 1)
                if pair.follows(1):
                    eng.wait_ge(vl_ready, 2 * (pair.n - 1) + g + 1)
                eng.copy(vf[:, g * NT:g * NT + NT, :].rearrange("p t h -> p (t h)"),
                         b[:, 0:NT * H]).then_inc(vf_ready, 1)

            def copy_permT(pair):
                eng.wait_ge(permT_ready, pair.n + 1)
                if pair.follows(2):
                    eng.wait_ge(z_ready, pair.n - 1)
                eng.copy(permT[pair.side][:, :, :].rearrange("p t n -> p (t n)"), bx3[:, :].bitcast(BF16)).then_inc(permT_copied, 1)

            def copy_y(pair):
                eng.wait_ge(y_ready, pair.n + 1)
                if pair.follows(1):
                    eng.wait_ge(z_ready, pair.n)
                eng.copy(y_sb[:, :, :].rearrange("p t o -> p (t o)"), by[:, 0:TILES * O]).then_inc(y_copied, 1)

            def sum_z(pair):
                eng.wait_ge(z_added, pair.n + 1)
                if pair.follows(1):
                    eng.wait_ge(mean_ready, pair.n)
                for c in range(TILES):
                    eng.activation(z_junk[:, c, :], z[:, c, :], ACT.Copy,
                                   accum_out=z_sum[:, c:c + 1]).then_inc(z_summed, 1)

            def sum_squares(pair):
                eng.wait_ge(centred_ready, pair.n + 1)
                for c in range(TILES):
                    eng.activation(z_junk[:, c, :], centred[:, c, :], ACT.Square,
                                   accum_out=spread[:, c:c + 1]).then_inc(squares_ready, 1)

            def deviation(pair):
                eng.wait_ge(squares_ready, TILES * (pair.n + 1))
                if pair.follows(1):
                    eng.wait_ge(rstd_ready, pair.n)
                eng.activation(std[:, :], spread[:, :], ACT.Sqrt, scale=1.0 / O,
                               bias=const("eps")).then_inc(std_ready, 1)

            def body(pair, order=True, prepare=True, turn=True, finish=True, settle=True):
                new, old, second = pair.at(1), pair.at(-1), pair.at(2)
                if order:
                    adj_signs(second)
                if turn:
                    copy_permT(pair)
                if order:
                    degrees(second, 0)
                if prepare:
                    copy_maskT(new)
                if prepare and not pair.general:
                    look_over(new)
                if prepare:
                    copy_slots(new)
                if order:
                    degrees(second, 1)
                if prepare:
                    copy_xs(new)
                if order:
                    copy_degrees(second)
                if settle:
                    sum_z(pair.at(-2))
                if prepare:
                    copy_u(new)
                if order:
                    high_x(second)
                    ranks(second)
                if settle:
                    sum_squares(pair.at(-2))
                    deviation(pair.at(-2))
                if prepare:
                    high_v(new, 0)
                    high_v(new, 1)
                if finish:
                    copy_y(old)
                if order:
                    middle_x(second)
                    permutation(second)

            first, next_one = Pair(0, 0), Pair(0, 1)
            degrees(first, 0)
            degrees(first, 1)
            copy_degrees(first)
            high_x(first)
            eng.wait_ge(consts_loaded["half"], 16)
            ranks(first)
            middle_x(first)
            copy_maskT(first)
            look_over(first)
            copy_slots(first)
            degrees(next_one, 0)
            copy_xs(first)
            degrees(next_one, 1)
            copy_degrees(next_one)
            copy_u(first)
            high_v(first, 0)
            high_v(first, 1)
            high_x(next_one)
            ranks(next_one)
            middle_x(next_one)
            body(first, finish=False, settle=False)
            body(next_one, settle=False)
            with eng.Fori(1, PAIRS // 2 - 1) as i:
                body(Pair(i, 0))
                body(Pair(i, 1))
            body(Pair(0, PAIRS - 2), order=False)
            body(Pair(0, PAIRS - 1), order=False, prepare=False)
            body(Pair(0, PAIRS), order=False, prepare=False, turn=False)
            body(Pair(0, PAIRS + 1), order=False, prepare=False, turn=False, finish=False)

            def general(pair):
                body(pair.at(-2), prepare=False, turn=False, finish=False, settle=False)
                body(pair.at(-1), order=False, turn=False, finish=False, settle=False)
                body(pair, order=False, prepare=False, finish=False, settle=False)
                body(pair.at(1), order=False, prepare=False, turn=False, settle=False)
                body(pair.at(2), order=False, prepare=False, turn=False, finish=False)

            general_loop(eng, general)

        @block.tensor
        def _(eng):
            eng.wait_ge(consts_ready, 2)
            eng.wait_ge(consts_loaded["row"], 16)

            def add_weights_up():
                eng.wait_ge(scale_step, 1)
                eng.matmul(ring[0][:, 0:2 * H], ones32[:, :], w_abs[:, :], start=True, stop=True).then_inc(w_sums_ready, 1)

            def turn_x_max():
                eng.wait_ge(scale_step, X_CHUNKS + 2)
                eng.matmul(ring[1][0:1, 0:P], x_max1[:, :], const("ident32"), start=True, stop=True).then_inc(x_turned, 1)

            def spread_x_top():
                eng.wait_ge(scale_step, X_CHUNKS + 4)
                eng.matmul(ring[2][:, 0:1], ones32[0:1, :], x_top[:, :], start=True, stop=True).then_inc(x_top_spread, 1)

            def keys(pair):
                eng.wait_ge(deg16_ready, pair.n + 1)
                if pair.follows(1):
                    eng.wait_ge(u_copied, 2 * pair.n)
                for c in range(TILES):
                    eng.matmul(bx0[:, c * P:c * P + P], deg16[pair.side][:, c:c + 1].to_broadcast([P, P]),
                               ident[:, :], start=True, stop=False)
                    last = eng.matmul(bx0[:, c * P:c * P + P], ones[0:1, :], tie_row[0:1, c * P:c * P + P],
                                      start=False, stop=True)
                last.then_inc(keys_ready, 1)

            def turn_masks(pair):
                eng.wait_ge(perm_ready, pair.n + 1)
                if pair.follows(1):
                    eng.wait_ge(vf_ready, 2 * pair.n)
                for g, b in enumerate((bx1, bx2)):
                    for k in range(NT):
                        for t in range(NT):
                            last = eng.matmul(b[:, k * N:k * N + N], mask[pair.side][:, g * NT + t, k * P:k * P + P],
                                              perm[pair.side][:, g * NT + t, :], start=(t == 0), stop=(t == NT - 1))
                    last.then_inc(maskT_ready, 1)

            def excesses(pair):
                if pair.follows(1):
                    eng.wait_ge(permT_copied, pair.n)
                for g in range(2):
                    for t in range(NT):
                        last = eng.matmul(bx3[:, g * N:g * N + N],
                                          deg16[pair.side][:, g * NT + t:g * NT + t + 1].to_broadcast([P, P]),
                                          perm[pair.side][:, g * NT + t, :], start=(t == 0),
                                          stop=(pair.general and t == NT - 1))
                    if not pair.general:
                        last = eng.matmul(bx3[:, g * N:g * N + N], ones[0:1, :], neg_given[0:1, g * N:g * N + N],
                                          start=False, stop=True)
                last.then_inc(excess_ready, 1)

            def number_slots(pair):
                for g, b in enumerate((bx0, bx1)):
                    eng.wait_ge(maskT_copied, 2 * pair.n + g + 1)
                    eng.matmul(b[:, 0:N], before[:, :], maskT[:, g * NT, :], start=True, stop=True)
                    eng.matmul(b[:, N:2 * N], ones[:, :], maskT[:, g * NT, :], start=True, stop=False)
                    eng.matmul(b[:, N:2 * N], before[:, :], maskT[:, g * NT + 1, :], start=False,
                               stop=True).then_inc(slots_ready, 1)

            def sort_x(pair):
                eng.wait_ge(xl_ready, pair.n + 1)
                eng.wait_ge(maskT_copied, 2 * pair.n + 2)
                steps = [(t, part) for t in range(NT) for part in (xh, xm, xl)]
                for s, (t, part) in enumerate(steps):
                    for g in range(2):
                        last = eng.matmul(bx2[g * F:g * F + F, 0:N], part[:, g * NT + t, :],
                                          perm[pair.side][:, g * NT + t, :], start=(s == 0),
                                          stop=(s == len(steps) - 1), skip_group_check=True)
                last.then_inc(xs_ready, 1)

            def hidden_u(pair):
                if not pair.follows(1):
                    eng.wait_ge(weights_ready, 4)
                eng.wait_ge(xs_copied, pair.n + 1)
                eng.wait_ge(slots_copied, 2 * pair.n + 1)
                for g in range(2):
                    last = eng.matmul(bx0[:, g * N:g * N + N], w1ab[:, g * P:g * P + P], xs[:, :], start=True,
                                      stop=True)
                last.then_inc(u_ready, 1)
                eng.wait_ge(slots_copied, 2 * pair.n + 2)
                eng.matmul(bx1[:, 0:N], w1ab[:, 2 * P:2 * H], xs[:, :], start=True, stop=True).then_inc(u_ready, 1)

            def hidden_v(pair):
                if not pair.follows(1):
                    eng.wait_ge(weights_ready, 10)
                eng.wait_ge(xT_loaded[pair.side], 16 * (pair.half + 1))
                eng.wait_ge(u_copied, 2 * (pair.n + 1))
                for t in range(NT):
                    for g, b in enumerate((bx1, bx2)):
                        rows = slice(g * F, g * F + F)
                        last = eng.matmul(b[:, t * H:t * H + H], xT_sb[pair.side][rows, t * P:t * P + P],
                                          w1n[rows, :], start=True, stop=True)
                        if t == NT - 1:
                            last.then_inc(v_ready, 1)

            def turn_perm(pair):
                eng.wait_ge(sums_started, 3 * (pair.n + 1))
                if not pair.general:
                    eng.wait_ge(over_ready, pair.n + 1)
                to = bx3[:, :].bitcast(BF16)
                for g in range(2):
                    for r in range(NT):
                        for t in range(NT):
                            at = (g * NT + r) * N + t * P
                            last = eng.transpose(to[:, at:at + P], perm[pair.side][:, g * NT + t, r * P:r * P + P],
                                                 ident[:, :])
                last.then_inc(permT_ready, 1)

            def project(pair):
                if pair.general:
                    eng.wait_ge(general_step, (pair.data + 1) * (N * GENERAL_STEPS))
                else:
                    for tile in ("main", "tail"):
                        eng.wait_ge(added[tile], ADDS[tile] * (pair.n + 1))
                if pair.follows(1):
                    eng.wait_ge(z_added, pair.n)
                for r in range(NT):
                    cols = slice(r * P, r * P + P)
                    to = by[:, r * 2 * O:(r + 1) * 2 * O]
                    for g in range(2):
                        eng.matmul(to[:, g * O:g * O + O], sm[pair.side][:, g, cols], w2ms[:, :],
                                   start=(g == 0), stop=False, skip_group_check=True)
                    last = eng.matmul(to, st[pair.side][:, cols], w2ts[:, :, :].rearrange("p g o -> p (g o)"),
                                      start=False, stop=True, skip_group_check=True)
                last.then_inc(y_ready, 1)

            def unsort_y(pair):
                eng.wait_ge(y_copied, pair.n + 1)
                eng.wait_ge(permT_copied, pair.n + 1)
                for g in range(2):
                    for t in range(NT):
                        at = TILES * O + (g * NT + t) * O
                        for r in range(NT):
                            last = eng.matmul(by[:, at:at + O], permT[pair.side][:, g * NT + r, t * P:t * P + P],
                                              y_sb[:, r * 2 + g, :], start=(r == 0), stop=(r == NT - 1))
                last.then_inc(z_ready, 1)

            def gather_into(side, b, tile, selection, n):
                steps = [(k, part) for k in range(NT) for part in (vh, vl)]
                if tile == "main":
                    for g in range(2):
                        for s, (k, part) in enumerate(steps):
                            last = eng.matmul(b[:, g * n:g * n + n], part[side][:, g * NT + k, 0:P],
                                              selection(g * NT + k), start=(s == 0), stop=(s == len(steps) - 1))
                else:
                    for s, (k, part) in enumerate(steps):
                        for g in range(2):
                            last = eng.matmul(b[g * HT:g * HT + HT, 0:n], part[side][:, g * NT + k, P:H],
                                              selection(g * NT + k), start=(s == 0), stop=(s == len(steps) - 1),
                                              skip_group_check=True)
                return last

            def gather(pair, unit):
                tile, s0, s1, _ = UNITS[unit]
                c0, n = unit_cols(unit)
                if unit == 0:
                    eng.wait_ge(vl_ready, 2 * (pair.n + 1))
                eng.wait_ge(hot_ready, NHOT * pair.n + min(s1, NHOT))
                if unit >= BANKS:
                    eng.wait_ge(shifted, NSHIFT * pair.n + SHIFTS_BEFORE[unit - BANKS + 1])
                else:
                    before_it = max(u for u in range(NU) if u % BANKS == unit)
                    if pair.follows(1):
                        eng.wait_ge(shifted, NSHIFT * (pair.n - 1) + SHIFTS_BEFORE[before_it + 1])
                b = ring[unit % BANKS]
                gather_into(pair.side, b, tile, lambda c: hot[pair.side][:, c, c0:c0 + n], n).then_inc(gathered, 1)

            def prepare_all(pair):
                turn_masks(pair)
                excesses(pair)
                if not pair.follows(1):
                    turn_x_max()
                number_slots(pair)
                if not pair.follows(1):
                    spread_x_top()
                sort_x(pair)
                hidden_u(pair)
                hidden_v(pair)

            def body(pair, order=True, prepare=True, finish=True):
                new, old, second = pair.at(1), pair.at(-1), pair.at(2)
                gather(pair, 0)
                turn_perm(pair)
                if prepare:
                    turn_masks(new)
                gather(pair, 1)
                if prepare:
                    excesses(new)
                gather(pair, 2)
                if prepare:
                    number_slots(new)
                gather(pair, 3)
                if prepare:
                    sort_x(new)
                gather(pair, 4)
                if prepare:
                    hidden_u(new)
                gather(pair, 5)
                if order:
                    keys(second)
                gather(pair, 6)
                gather(pair, 7)
                gather(pair, 8)
                if prepare:
                    hidden_v(new)
                if finish:
                    project(old)
                gather(pair, 9)
                gather(pair, 10)
                if finish:
                    unsort_y(old)

            keys(Pair(0, 0))
            add_weights_up()
            prepare_all(Pair(0, 0))
            keys(Pair(0, 1))
            body(Pair(0, 0), finish=False)
            body(Pair(0, 1))
            with eng.Fori(1, PAIRS // 2 - 1) as i:
                body(Pair(i, 0))
                body(Pair(i, 1))
            body(Pair(0, PAIRS - 2), order=False)
            body(Pair(0, PAIRS - 1), order=False, prepare=False)
            project(Pair(0, PAIRS - 1))
            unsort_y(Pair(0, PAIRS - 1))

            def general(pair):
                keys(pair)
                prepare_all(pair)
                with eng.Fori(0, N) as s:
                    eng.wait_ge(vl_ready, 2 * (pair.n + 1))
                    eng.wait_ge(general_hot, pair.data * N + s + 1)
                    gather_into(pair.side, ring[0], "main", lambda c: hot[0][:, c, 0:N], N)
                    gather_into(pair.side, ring[1], "tail", lambda c: hot[0][:, c, 0:N], N
                                ).then_inc(general_gathered, 1)
                project(pair)
                turn_perm(pair)
                unsort_y(pair)

            general_loop(eng, general)

        @block.vector
        def _(eng):
            eng.memset(over_sum[:, :], 0.0).then_inc(over_added, 1)
            eng.memset(ones32[:, :], 1.0).then_inc(weights_ready, 1)
            eng.memset(ones[:, :], 1.0).then_inc(consts_ready, 1)

            def positive_adj(pair):
                eng.wait_ge(adj_loaded[pair.side], 16 * (pair.half + 1))
                if pair.follows(1):
                    eng.wait_ge(degrees_ready, TILES * pair.n)
                eng.tensor_scalar(adj_sign[:, :, :], adj_sb[pair.side][:, :, :], 0.0, None,
                                  ALU.is_gt).then_inc(signs_ready, 1)

            def permutation(pair):
                eng.wait_ge(ranks_ready, pair.n + 1)
                for c in range(TILES):
                    last = eng.tensor_scalar(perm[pair.side][:, c, :], signs, rank[:, c:c + 1], None,
                                             ALU.is_equal)
                last.then_inc(perm_ready, 1)

            def low_v(pair, g):
                eng.wait_ge(vf_ready, 2 * pair.n + g + 1)
                c = slice(g * NT, g * NT + NT)
                eng.tensor_tensor(vl[pair.side][:, c, :], vf[:, c, :], vh[pair.side][:, c, :],
                                  ALU.subtract).then_inc(vl_ready, 1)

            def absolute_weights():
                eng.wait_ge(weights_loaded, 16)
                eng.scalar_tensor_tensor(out=w_abs[:, :], in0=w1b, scalar=-1.0, in1=w1b,
                                         op0=ALU.mult, op1=ALU.max).then_inc(scale_step, 1)
                eng.tensor_tensor(w1s[:, :], w1a, w1b, ALU.add).then_inc(w1s_ready, 1)

            def chunk_max(c):
                eng.wait_ge(x_all_loaded[c], 16)
                eng.tensor_reduce(x_max[:, c:c + 1], x_all[:, c, :], AX.X, ALU.max,
                                  apply_absolute_value=True).then_inc(scale_step, 1)

            def scale_weights(next_one):
                eng.wait_ge(scale_step, X_CHUNKS + 1)
                eng.tensor_reduce(x_max1[:, :], x_max[:, :], AX.X, ALU.max).then_inc(scale_step, 1)
                eng.wait_ge(w_sums_ready, 1)
                eng.tensor_reduce(w_top[:, :], ring[0][:, 0:2 * H], AX.X, ALU.max).then_inc(scale_step, 1)
                positive_adj(next_one)
                eng.wait_ge(x_turned, 1)
                eng.tensor_reduce(x_top[:, :], ring[1][0:1, 0:P], AX.X, ALU.max).then_inc(scale_step, 1)
                eng.wait_ge(x_top_spread, 1)
                eng.wait_ge(scale_step, X_CHUNKS + 4)
                eng.tensor_tensor(bound[:, :], ring[2][:, 0:1], w_top[:, :], ALU.mult).then_inc(scale_step, 1)
                eng.wait_ge(scale_step, X_CHUNKS + 5)
                eng.tensor_scalar(bound1[:, :], bound[:, :], LEAST_BOUND, None, ALU.max).then_inc(scale_step, 1)
                eng.wait_ge(scale_step, X_CHUNKS + 6)
                eng.tensor_scalar(power[:, :], bound1[:, :].bitcast(I32), EXPONENT, None,
                                  ALU.bitwise_and).then_inc(scale_step, 1)
                eng.wait_ge(scale_step, X_CHUNKS + 7)
                eng.tensor_scalar(up_bits[:, :], power[:, :], -1.0, float((2 * BIAS + TOP - 1) << MANTISSA),
                                  ALU.mult, ALU.add).then_inc(scale_step, 1)
                eng.tensor_scalar(down[:, :], power[:, :].bitcast(F32), 2.0 ** (1 - TOP), None,
                                  ALU.mult).then_inc(scale_step, 1)
                eng.wait_ge(scale_step, X_CHUNKS + 9)
                eng.wait_ge(w1s_ready, 1)
                up = up_bits[:, :].bitcast(F32)
                eng.tensor_scalar(w1ab[:, :], w1s[:, :], up, None, ALU.mult).then_inc(weights_ready, 1)
                eng.tensor_scalar(b1ms[:, :], b1m, up, None, ALU.mult).then_inc(weights_ready, 1)
                eng.tensor_scalar(b1ts[:, :], b1t, up, None, ALU.mult).then_inc(weights_ready, 1)
                for g in range(2):
                    rows = slice(g * F, g * F + F)
                    for to, at, n in ((0, g * P, P), (P, 2 * P + g * HT, HT)):
                        eng.tensor_scalar(w1n[rows, to:to + n], w1b[rows, at:at + n], up[rows, :], -1.0, ALU.mult,
                                          ALU.mult).then_inc(weights_ready, 1)
                eng.tensor_scalar(w2ms[:, :], w2m, down[:, 0:1], None, ALU.mult).then_inc(weights_ready, 1)
                eng.tensor_scalar(w2ts[:, :, :], w2t, down[:, 0:1], None, ALU.mult).then_inc(weights_ready, 1)

            def start_sums(pair):
                eng.wait_ge(u_copied, 2 * (pair.n + 1))
                eng.wait_ge(excess_ready, pair.n + 1)
                if not pair.general:
                    eng.wait_ge(over_ready, pair.n + 1)
                if pair.follows(2):
                    eng.wait_ge(y_ready, pair.n - 1)
                side = pair.side
                if pair.general:
                    eng.memset(sm[side][:, :, :], 0.0).then_inc(sums_started, 2)
                    eng.memset(st[side][:, :], 0.0).then_inc(sums_started, 1)
                    return
                eng.scalar_tensor_tensor(out=sm[side][:, :, :].rearrange("p g r -> p (g r)"),
                                         in0=um[side][:, :, :].rearrange("p g r -> p (g r)"), scalar=0.0,
                                         in1=bx3[:, :], op0=ALU.max, op1=ALU.mult).then_inc(sums_started, 1)
                for g in range(2):
                    rows = slice(g * HT, g * HT + HT)
                    eng.scalar_tensor_tensor(out=st[side][rows, :], in0=ut[side][rows, :], scalar=0.0,
                                             in1=bx3[rows, g * N:g * N + N], op0=ALU.max,
                                             op1=ALU.mult).then_inc(sums_started, 1)

            def selections(pair, first, last):
                if first == 0:
                    eng.wait_ge(slots_copied, 2 * (pair.n + 1))
                    if pair.follows(2):
                        eng.wait_ge(gathered, NU * (pair.n - 1))
                side = pair.side
                for s in range(first, last):
                    c0, n = START[s], CAPS[s]
                    if s < BIG_SLOTS:
                        eng.tensor_scalar(hot[side][:, :, c0:c0 + n], slotT[:, :, 0:n], float(MARK + s), None,
                                          ALU.is_equal).then_inc(hot_ready, 1)
                    else:
                        eng.tensor_tensor(
                            hot[side][:, :, c0:].rearrange("p c (s r) -> p c s r", r=SMALL),
                            slotT[:, :, 0:SMALL].unsqueeze(2).broadcast_to([P, TILES, NSMALL, SMALL]),
                            small_marks[:, :].rearrange("p (s r) -> p s r", r=SMALL).unsqueeze(1)
                            .broadcast_to([P, TILES, NSMALL, SMALL]),
                            ALU.is_equal).then_inc(hot_ready, 1)

            def views(pair, unit, segment, b, start=0):
                tile, s0, _, _ = UNITS[unit]
                _, n = unit_cols(unit)
                first, slots = segment
                c = START[first] - START[s0]
                cap = CAPS[first]
                if tile == "main":
                    v = b[:, 0:2 * n].rearrange("p (g c) -> p g c", g=2)[:, :, c:c + slots * cap]
                    return v.rearrange("p g (s r) -> p g s r", r=cap)
                return b[:, c:c + slots * cap].rearrange("p (s r) -> p s r", r=cap)

            def shift(pair, unit):
                tile = UNITS[unit][0]
                side = pair.side
                eng.wait_ge(gathered, NU * pair.n + unit + 1)
                b, to = ring[unit % BANKS], tmp[unit % NTMP]
                for first, slots in UNITS[unit][3]:
                    cap = CAPS[first]
                    if tile == "main":
                        u = um[side][:, :, 0:cap].unsqueeze(2).broadcast_to([P, 2, slots, cap])
                    else:
                        u = ut[side][:, 0:cap].unsqueeze(1).broadcast_to([P, slots, cap])
                    eng.tensor_tensor(views(pair, unit, (first, slots), to), views(pair, unit, (first, slots), b),
                                      u, ALU.add).then_inc(shifted, 1)

            def add(pair, unit, segment=0, part=None):
                tile = UNITS[unit][0]
                side = pair.side
                sums = sm[side] if tile == "main" else st[side]
                first, slots = UNITS[unit][3][segment]
                eng.wait_ge(shifted, NSHIFT * pair.n + SHIFTS_BEFORE[unit] + segment + 1)
                if unit == 0:
                    eng.wait_ge(sums_started, 3 * (pair.n + 1))
                done = ADDS_BEFORE[unit] + sum(n for _, n in UNITS[unit][3][:segment])
                cap = CAPS[first]
                v = views(pair, unit, (first, slots), tmp[unit % NTMP])
                done += part or 0
                for s in range(slots) if part is None else (part,):
                    to = sums[:, :, 0:cap] if tile == "main" else sums[:, 0:cap]
                    if done or pair.follows(1):
                        eng.wait_ge(added[tile], ADDS[tile] * pair.n + done)
                    eng.scalar_tensor_tensor(out=to, in0=v[:, :, s, :] if tile == "main" else v[:, s, :],
                                             scalar=0.0, in1=to, op0=ALU.max, op1=ALU.add).then_inc(added[tile], 1)
                    done += 1

            def small_views(pair, unit):
                side = pair.side
                v = views(pair, unit, (BIG_SLOTS, NSMALL), tmp[unit % NTMP])
                if UNITS[unit][0] == "main":
                    return v, v.rearrange("p g s r -> p g r s"), small_sum[:, :, :], sm[side][:, :, 0:SMALL], 1
                return v, v.rearrange("p s r -> p r s"), small_sum_t[:, :], st[side][:, 0:SMALL], 0

            def clamp_small(pair, unit):
                v, _, _, _, k = small_views(pair, unit)
                eng.wait_ge(shifted, NSHIFT * pair.n + SHIFTS_BEFORE[unit + 1])
                eng.tensor_scalar(v, v, 0.0, None, ALU.max).then_inc(clamped, 1)

            def reduce_small(pair, unit):
                _, turned, part, _, k = small_views(pair, unit)
                eng.wait_ge(clamped, 2 * pair.n + k + 1)
                eng.tensor_reduce(part, turned, AX.X, ALU.add).then_inc(reduced, 1)

            def add_small(pair, unit):
                _, _, part, to, k = small_views(pair, unit)
                eng.wait_ge(reduced, 2 * pair.n + k + 1)
                tile = UNITS[unit][0]
                eng.wait_ge(added[tile], ADDS[tile] * (pair.n + 1) - 1)
                eng.tensor_tensor(to, to, part, ALU.add).then_inc(added[tile], 1)

            def add_residual(pair):
                eng.wait_ge(z_ready, pair.n + 1)
                eng.wait_ge(xb_ready, pair.n + 1)
                if pair.follows(1):
                    eng.wait_ge(centred_ready, pair.n)
                zf = z[:, :, :].rearrange("p t o -> p (t o)")
                eng.tensor_tensor(zf, by[:, TILES * O:2 * TILES * O],
                                  xb[pair.side][:, :, :].rearrange("p t f -> p (t f)"), ALU.add).then_inc(z_added, 1)

            def inverse_deviation(pair):
                eng.wait_ge(std_ready, pair.n + 1)
                if pair.follows(1):
                    eng.wait_ge(normed, pair.n)
                eng.reciprocal(rstd[:, :], std[:, :]).then_inc(rstd_ready, 1)

            def body(pair, order=True, prepare=True, finish=True, settle=True):
                new, old, older = pair.at(1), pair.at(-1), pair.at(-2)
                shift(pair, 0)
                shift(pair, 1)
                add(pair, 0)
                add(pair, 1, 0, 0)
                shift(pair, 2)
                add(pair, 1, 0, 1)
                add(pair, 2)
                shift(pair, 3)
                add(pair, 3, 0)
                shift(pair, 4)
                add(pair, 3, 1)
                if prepare:
                    selections(new, 0, 1)
                add(pair, 4)
                shift(pair, 5)
                add(pair, 5, 0)
                if prepare:
                    selections(new, 1, 2)
                add(pair, 5, 1)
                shift(pair, 6)
                add(pair, 5, 2)
                if prepare:
                    selections(new, 2, 3)
                shift(pair, 7)
                add(pair, 6)
                if prepare:
                    selections(new, 3, 5)
                add(pair, 7)
                shift(pair, 8)
                add(pair, 8, 0, 0)
                if prepare:
                    selections(new, 5, 6)
                add(pair, 8, 0, 1)
                if settle:
                    inverse_deviation(older)
                clamp_small(pair, 8)
                if prepare:
                    start_sums(new)
                shift(pair, 9)
                add(pair, 9, 0)
                reduce_small(pair, 8)
                if prepare:
                    selections(new, 6, 7)
                add(pair, 9, 1)
                shift(pair, 10)
                add_small(pair, 8)
                add(pair, 10, 0, 0)
                clamp_small(pair, 10)
                if prepare:
                    selections(new, 7, 8)
                add(pair, 10, 0, 1)
                reduce_small(pair, 10)
                if finish:
                    add_residual(old)
                if prepare:
                    selections(new, 8, 9)
                add_small(pair, 10)
                if prepare:
                    selections(new, 9, NHOT)

            first, next_one = Pair(0, 0), Pair(0, 1)
            positive_adj(first)
            eng.wait_ge(consts_loaded["half"], 16)
            eng.tensor_copy(ident[:, :], const("ident16")).then_inc(consts_ready, 1)
            absolute_weights()
            chunk_max(0)
            permutation(first)
            for c in range(1, X_CHUNKS):
                chunk_max(c)
            scale_weights(next_one)
            selections(first, 0, 3)
            start_sums(first)
            selections(first, 3, 8)
            low_v(first, 1)
            selections(first, 8, NHOT)
            permutation(next_one)
            body(first, finish=False, settle=False)
            body(next_one, settle=False)
            with eng.Fori(1, PAIRS // 2 - 1) as i:
                body(Pair(i, 0))
                body(Pair(i, 1))
            body(Pair(0, PAIRS - 2), order=False)
            body(Pair(0, PAIRS - 1), order=False, prepare=False)
            inverse_deviation(Pair(0, PAIRS - 2))
            add_residual(Pair(0, PAIRS - 1))
            inverse_deviation(Pair(0, PAIRS - 1))

            def general(pair):
                side = pair.side
                start_sums(pair)
                sf = sm[side][:, :, :].rearrange("p g r -> p (g r)")
                uf = um[side][:, :, :].rearrange("p g r -> p (g r)")
                tail = tmp[1][:, 0:N]
                eng.wait_ge(consts_loaded["general"], 16)
                with eng.Fori(0, N) as s:
                    number = pair.data * N + s
                    done = number * GENERAL_STEPS
                    mark = const("marks")[:, bass.ds(s, 1)]
                    slot = const("iota")[:, bass.ds(s, 1)]
                    eng.wait_ge(slots_copied, 2 * (pair.n + 1))
                    eng.wait_ge(sums_started, 3 * (pair.n + 1))
                    eng.tensor_scalar(hot[0][:, :, 0:N], slotT[:, :, :], mark, None,
                                      ALU.is_equal).then_inc(general_hot, 1)
                    eng.wait_ge(general_gathered, number + 1)
                    eng.tensor_tensor(tmp[0][:, :], ring[0][:, :], uf, ALU.add).then_inc(general_step, 1)
                    eng.tensor_tensor(tail, ring[1][:, 0:N], ut[side][:, :], ALU.add).then_inc(general_step, 1)
                    eng.wait_ge(general_step, done + 2)
                    eng.scalar_tensor_tensor(out=tmp[0][:, :], in0=bx3[:, :], scalar=slot, in1=tmp[0][:, :],
                                             op0=ALU.is_gt, op1=ALU.mult).then_inc(general_step, 1)
                    for g in range(2):
                        rows = slice(g * HT, g * HT + HT)
                        eng.scalar_tensor_tensor(out=tail[rows, :], in0=bx3[rows, g * N:g * N + N],
                                                 scalar=slot[rows, :], in1=tail[rows, :],
                                                 op0=ALU.is_gt, op1=ALU.mult).then_inc(general_step, 1)
                    eng.wait_ge(general_step, done + 5)
                    eng.scalar_tensor_tensor(out=sf, in0=tmp[0][:, :], scalar=0.0, in1=sf,
                                             op0=ALU.max, op1=ALU.add).then_inc(general_step, 1)
                    eng.scalar_tensor_tensor(out=st[side][:, :], in0=tail, scalar=0.0, in1=st[side][:, :],
                                             op0=ALU.max, op1=ALU.add).then_inc(general_step, 1)
                    eng.wait_ge(general_step, done + GENERAL_STEPS)
                    eng.tensor_copy(idle[:, :], std[:, 0:1])
                add_residual(pair)
                inverse_deviation(pair)

            general_loop(eng, general)


def kernel(**inputs):
    import concourse.bacc as bacc
    from concourse.bass_utils import run_bass_kernel_spmd

    nc = bacc.Bacc("TRN2", target_bir_lowering=False, num_devices=1)
    x = np.ascontiguousarray(inputs["x"])
    arrays = {
        "x": x,
        "xT": np.ascontiguousarray(x.reshape(PAIRS, 2, N, F).transpose(0, 1, 3, 2).reshape(PAIRS, 2 * F, N)),
        "adj": np.ascontiguousarray(inputs["adj"]),
        "weights": lay_out_weights(*(np.asarray(inputs["L0_gnn_" + k]) for k in ("W1", "b1", "W2", "b2"))),
        **constants(),
    }
    args = [nc.dram_tensor(name, a.shape, mybir.dt.from_np(a.dtype), kind="ExternalInput").ap()
            for name, a in arrays.items()]
    out = nc.dram_tensor("out", (GRAPHS, N, F), F32, kind="ExternalOutput").ap()
    build(nc, *args, out)
    return run_bass_kernel_spmd(nc, [arrays], core_ids=[0]).results[0]["out"]
```
